# Optimizing a Trainium2 kernel written in Bass

```python
import numpy as np
import jax
import jax.numpy as jnp

def _softmax(x, axis=-1):
    return jax.nn.softmax(x, axis=axis)

def _gelu(x):
    return jax.nn.gelu(x, approximate=True)

def _silu(x):
    return jax.nn.silu(x)

def _sigmoid(x):
    return jax.nn.sigmoid(x)

def _layernorm(x, axis=-1, eps=1e-05):
    m = jnp.mean(x, axis=axis, keepdims=True)
    v = jnp.var(x, axis=axis, keepdims=True)
    return (x - m) / jnp.sqrt(v + eps)

def _scatter_add(tgt, idx, src, axis=0):
    return tgt.at[idx].add(src)

def _segment_sum(src, seg, n):
    return jax.ops.segment_sum(src, seg, n)
kernel_name = 'mk_adaln_d1_jaxref_r8_897bd7'

def setup_inputs(seed: int=0):
    np.random.seed(seed)
    _w = jnp.asarray

    def _L0_attn_setup():
        import jax, jax.numpy as jnp
        import numpy as np
        B, T, HID = (4, 256, 128)
        H, D, V = (8, 64, 128)
        EPS = 1e-05

        def _rotary(x, T, D):
            inv_freq = 1.0 / 10000.0 ** (jnp.arange(0, D, 2, dtype=jnp.float32) / D)
            t = jnp.arange(T, dtype=jnp.float32)
            freqs = t[:, None] * inv_freq[None, :]
            emb = jnp.concatenate([freqs, freqs], axis=-1)
            cos = jnp.cos(emb)[None, None, :, :]
            sin = jnp.sin(emb)[None, None, :, :]
            x1, x2 = jnp.split(x, 2, axis=-1)
            rot = jnp.concatenate([-x2, x1], axis=-1)
            return x * cos + rot * sin
        key = jax.random.key(seed)
        ks = jax.random.split(key, 7)
        sc = 0.02
        return {'x': jax.random.normal(ks[0], (B, T, HID), dtype=jnp.float32), 'Wq': jax.random.normal(ks[1], (H * D, HID), dtype=jnp.float32) * sc, 'Wk': jax.random.normal(ks[2], (H * D, HID), dtype=jnp.float32) * sc, 'Wv': jax.random.normal(ks[3], (H * V, HID), dtype=jnp.float32) * sc, 'Wg': jax.random.normal(ks[4], (H * V, HID), dtype=jnp.float32) * sc, 'Wo': jax.random.normal(ks[5], (HID, H * V), dtype=jnp.float32) * sc, 'gn_weight': jnp.ones((H * V,), dtype=jnp.float32), 'gn_bias': jnp.zeros((H * V,), dtype=jnp.float32)}
    _L0_attn_in = _L0_attn_setup()

    def _L0_ffn_setup():
        import jax, jax.numpy as jnp
        import numpy as np
        DIM = 128

        def _reference_tuple_inner(x, W_r, W_k, W_v, mu_r, mu_k):
            B, T, C = x.shape
            x_prev = jnp.concatenate([jnp.zeros((B, 1, C), x.dtype), x[:, :-1, :]], axis=1)
            xr = mu_r * x + (1.0 - mu_r) * x_prev
            xk = mu_k * x + (1.0 - mu_k) * x_prev
            r = jax.nn.sigmoid(jnp.einsum('btc,dc->btd', xr, W_r))
            k = jnp.einsum('btc,dc->btd', xk, W_k)
            k_act = jnp.square(jax.nn.relu(k))
            out = r * jnp.einsum('btc,dc->btd', k_act, W_v)
            new_state = x[:, -1, :]
            return (out, new_state)
        key = jax.random.key(seed)
        ks = jax.random.split(key, 6)
        B, T, C = (8, 256, DIM)
        x = jax.random.normal(ks[0], (B, T, C), dtype=jnp.float32)
        s = 1.0 / np.sqrt(C)
        W_r = jax.random.uniform(ks[1], (C, C), jnp.float32, -s, s)
        W_k = jax.random.uniform(ks[2], (C, C), jnp.float32, -s, s)
        W_v = jax.random.uniform(ks[3], (C, C), jnp.float32, -s, s)
        mu_r = jax.random.uniform(ks[4], (C,), jnp.float32)
        mu_k = jax.random.uniform(ks[5], (C,), jnp.float32)
        return {'x': x, 'W_r': W_r, 'W_k': W_k, 'W_v': W_v, 'mu_r': mu_r, 'mu_k': mu_k}
    _L0_ffn_in = _L0_ffn_setup()
    _L0_c = _w((lambda *s: np.random.randn(*s).astype(np.float32) * 0.05)(8, 128))
    _L0_wmod = _w((lambda *s: np.random.randn(*s).astype(np.float32) * 0.05)(128, 6 * 128) * 128 ** (-0.5))
    _d = {'L0_attn_x': _L0_attn_in['x'], 'L0_attn_Wq': _L0_attn_in['Wq'], 'L0_attn_Wk': _L0_attn_in['Wk'], 'L0_attn_Wv': _L0_attn_in['Wv'], 'L0_attn_Wg': _L0_attn_in['Wg'], 'L0_attn_Wo': _L0_attn_in['Wo'], 'L0_attn_gn_weight': _L0_attn_in['gn_weight'], 'L0_attn_gn_bias': _L0_attn_in['gn_bias'], 'L0_ffn_W_r': _L0_ffn_in['W_r'], 'L0_ffn_W_k': _L0_ffn_in['W_k'], 'L0_ffn_W_v': _L0_ffn_in['W_v'], 'L0_ffn_mu_r': _L0_ffn_in['mu_r'], 'L0_ffn_mu_k': _L0_ffn_in['mu_k'], 'L0_c': _L0_c, 'L0_wmod': _L0_wmod}
    _x0 = _d['L0_attn_x']
    _d['L0_attn_x'] = jax.random.normal(jax.random.fold_in(jax.random.key(seed), 1), (8, 1024, 128), dtype=_x0.dtype)
    del _x0
    return _d

def reference(L0_attn_x, L0_attn_Wq, L0_attn_Wk, L0_attn_Wv, L0_attn_Wg, L0_attn_Wo, L0_attn_gn_weight, L0_attn_gn_bias, L0_ffn_W_r, L0_ffn_W_k, L0_ffn_W_v, L0_ffn_mu_r, L0_ffn_mu_k, L0_c, L0_wmod):

    def _L0_attn_ref(x, Wq, Wk, Wv, Wg, Wo, gn_weight, gn_bias):
        import jax, jax.numpy as jnp
        import numpy as np
        B, T, HID = (4, 256, 128)
        H, D, V = (8, 64, 128)
        EPS = 1e-05

        def _rotary(x, T, D):
            inv_freq = 1.0 / 10000.0 ** (jnp.arange(0, D, 2, dtype=jnp.float32) / D)
            t = jnp.arange(T, dtype=jnp.float32)
            freqs = t[:, None] * inv_freq[None, :]
            emb = jnp.concatenate([freqs, freqs], axis=-1)
            cos = jnp.cos(emb)[None, None, :, :]
            sin = jnp.sin(emb)[None, None, :, :]
            x1, x2 = jnp.split(x, 2, axis=-1)
            rot = jnp.concatenate([-x2, x1], axis=-1)
            return x * cos + rot * sin
        Bx, Tx, _ = x.shape
        q = jnp.einsum('bti,oi->bto', x, Wq).reshape(Bx, Tx, H, D).transpose(0, 2, 1, 3)
        k = jnp.einsum('bti,oi->bto', x, Wk).reshape(Bx, Tx, H, D).transpose(0, 2, 1, 3)
        v = jnp.einsum('bti,oi->bto', x, Wv).reshape(Bx, Tx, H, V).transpose(0, 2, 1, 3)
        g = jnp.einsum('bti,oi->bto', x, Wg)
        q = _rotary(q, Tx, D)
        k = _rotary(k, Tx, D)
        gamma = 1.0 - jnp.exp2(-5.0 - jnp.arange(H, dtype=jnp.float32))
        s = jnp.log2(gamma)
        n = jnp.arange(Tx, dtype=jnp.float32)
        rel = n[:, None] - n[None, :]
        causal = rel >= 0
        decay = jnp.where(causal[None, :, :], jnp.exp2(rel[None, :, :] * s[:, None, None]), 0.0)
        scores = jnp.einsum('bhtd,bhsd->bhts', q, k) * D ** (-0.5)
        scores = scores * decay[None]
        o = jnp.einsum('bhts,bhsv->bhtv', scores, v)
        o = o.transpose(0, 2, 1, 3)
        mean = jnp.mean(o, axis=-1, keepdims=True)
        var = jnp.var(o, axis=-1, keepdims=True)
        o = (o - mean) * jax.lax.rsqrt(var + EPS)
        o = o * gn_weight.reshape(H, V) + gn_bias.reshape(H, V)
        o = o.reshape(Bx, Tx, H * V)
        o = o * jax.nn.silu(g)
        return jnp.einsum('btc,oc->bto', o, Wo)

    def _L0_ffn_ref(x, W_r, W_k, W_v, mu_r, mu_k):
        import jax, jax.numpy as jnp
        import numpy as np
        DIM = 128

        def _reference_tuple_inner(x, W_r, W_k, W_v, mu_r, mu_k):
            B, T, C = x.shape
            x_prev = jnp.concatenate([jnp.zeros((B, 1, C), x.dtype), x[:, :-1, :]], axis=1)
            xr = mu_r * x + (1.0 - mu_r) * x_prev
            xk = mu_k * x + (1.0 - mu_k) * x_prev
            r = jax.nn.sigmoid(jnp.einsum('btc,dc->btd', xr, W_r))
            k = jnp.einsum('btc,dc->btd', xk, W_k)
            k_act = jnp.square(jax.nn.relu(k))
            out = r * jnp.einsum('btc,dc->btd', k_act, W_v)
            new_state = x[:, -1, :]
            return (out, new_state)
        return _reference_tuple_inner(x, W_r, W_k, W_v, mu_r, mu_k)[0]
    x = L0_attn_x
    mod = (_silu(L0_c) @ L0_wmod).reshape(L0_c.shape[0], 6, 1, -1)
    sa, ca, ga, sb, cb, gb = (mod[:, 0], mod[:, 1], mod[:, 2], mod[:, 3], mod[:, 4], mod[:, 5])
    ga = (2 * (ga >= 0) - 1) * jnp.maximum(jnp.abs(ga), 0.25)
    gb = (2 * (gb >= 0) - 1) * jnp.maximum(jnp.abs(gb), 0.25)
    h = _layernorm(x, axis=-1) * (1 + ca) + sa
    x = x + ga * _L0_attn_ref(h, L0_attn_Wq, L0_attn_Wk, L0_attn_Wv, L0_attn_Wg, L0_attn_Wo, L0_attn_gn_weight, L0_attn_gn_bias)
    h = _layernorm(x, axis=-1) * (1 + cb) + sb
    x = x + gb * _L0_ffn_ref(h, L0_ffn_W_r, L0_ffn_W_k, L0_ffn_W_v, L0_ffn_mu_r, L0_ffn_mu_k)
    return x

_drawn_inputs = setup_inputs


def setup_inputs(seed=0):
    import zlib

    import numpy as np

    out = dict(_drawn_inputs(seed))
    spreads = {'L0_attn_gn_weight': (1.0, 0.6), 'L0_attn_gn_bias': (0.0, 0.8)}
    factors = {'L0_attn_Wq': 2.949,
     'L0_attn_Wk': 2.941,
     'L0_attn_Wv': 2.947,
     'L0_attn_Wg': 2.941,
     'L0_attn_Wo': 2.93,
     'L0_ffn_W_r': 8.0,
     'L0_ffn_W_k': 2.98,
     'L0_ffn_W_v': 2.754,
     'L0_ffn_mu_r': 8.0,
     'L0_ffn_mu_k': 4.645}
    for name, (base, spread) in spreads.items():
        noise = np.random.default_rng([zlib.crc32(name.encode()), seed]).standard_normal(out[name].shape)
        drawn = base * np.exp(spread * noise) if base else spread * noise
        out[name] = jnp.asarray(drawn.astype(out[name].dtype))
    for name, factor in factors.items():
        out[name] = (out[name] * factor).astype(out[name].dtype)
    return out
```

```python
from contextlib import ExitStack

import numpy as np

import concourse.bass as bass
from concourse import mybir

F32 = mybir.dt.float32
F32R = mybir.dt.float32r
ALU = mybir.AluOpType
ACT = mybir.ActivationFunctionType

P = 128
B, T, C = 8, 1024, 128
H, D, V = 8, 64, 128
PAIRS = H // 2
GC = 4
NCHUNK = B * T // P
NGROUP = NCHUNK // GC
CB = T // P
GB = CB // GC
W = GC * P
EPS = 1e-5
MID = T // 2

NX, NHT, NHN, NMOD, NN = 5, 3, 2, 3, 2 * GC


def constants():
    inv_freq = (np.float32(1.0) / np.float32(10000.0) ** (np.arange(0, D, 2, dtype=np.float32) / np.float32(D)))
    angle = (np.arange(T, dtype=np.float32)[:, None] * inv_freq.astype(np.float32)[None, :]).astype(np.float32)
    cos, sin = np.cos(angle), np.sin(angle)
    rotary = np.stack([np.concatenate([cos, cos], 1), np.concatenate([-sin, sin], 1)], 1)
    gamma = 1.0 - np.exp2(-5.0 - np.arange(H, dtype=np.float64))
    away = MID - np.arange(T, dtype=np.float64)
    key_decay = gamma[None, :] ** away[:, None]
    norm_eps = EPS * D * key_decay ** 2
    causal = (np.arange(P)[:, None] <= np.arange(P)[None, :])
    by_partition = lambda a: a.reshape(CB, P, -1).transpose(1, 0, 2).reshape(P, -1)
    parts = [by_partition(rotary), by_partition(key_decay), by_partition(norm_eps), causal, np.eye(P)]
    return np.ascontiguousarray(np.concatenate(parts, 1).astype(np.float32))


def build(nc, x, cT, w_mod, w_qkT, w_gT, w_vT, w_oT, norm_wb, w_ffnT, ffn_mu, const, out):
    with ExitStack() as ctx:
        def sb(name, shape, dt=F32):
            return ctx.enter_context(nc.sbuf_tensor(name, shape, dt))

        n_const = const.shape[1]
        consts = sb("consts", [P, n_const])
        at = [0]

        def const_part(n):
            at[0] += n
            return consts[:, at[0] - n:at[0]]

        rotary = const_part(CB * 2 * D).rearrange("p (c k d) -> p c k d", c=CB, k=2)
        key_decay = const_part(CB * H).rearrange("p (c h) -> p c h", c=CB)
        norm_eps = const_part(CB * H).rearrange("p (c h) -> p c h", c=CB)
        causal = const_part(P)
        ident = const_part(P)

        X = sb("X", [P, NX, GC, C])
        kcos = sb("kcos", [P, CB, H, D])
        ksin = sb("ksin", [P, CB, H, D])
        wqk = {s: sb("wqk_" + s, [P, 2 * H * D], F32R) for s in ("hi", "lo")}
        wg = {s: sb("wg_" + s, [P, H * V], F32R) for s in ("hi", "lo")}
        wv = sb("wv", [P, H, V])
        wo = sb("wo", [P, H, C])
        wffn = sb("wffn", [P, 3, C])
        mu = sb("mu", [P, 2])
        gn = sb("gn", [P, 2, H])
        wmod = sb("wmod", [P, 6 * C])
        cond = sb("cond", [P, B])
        silu_c = sb("silu_c", [P, B])
        silu_rows = sb("silu_rows", [P, P])
        mod = sb("mod", [P, NMOD, 4, C])
        mod_pos = sb("mod_pos", [P, 2, C])
        mod_neg = sb("mod_neg", [P, 2, C])
        mod_cols = sb("mod_cols", [P, 2, B])
        minus_half = sb("minus_half", [P, 1])
        eps = sb("eps", [P, 1])

        ln_stats = sb("ln_stats", [P, 2, GC, 6])
        ln_mv = sb("ln_mv", [P, 2, GC, 2])
        ln_var = sb("ln_var", [P, 2, GC])
        ln_rstd = sb("ln_rstd", [P, 2, GC])
        normed = sb("normed", [P, GC, C])
        normed2 = sb("normed2", [P, GC, C])
        h_nat = sb("h_nat", [P, NHN, GC, C])
        hT = {s: sb("hT_" + s, [P, NHT, W], F32R) for s in ("hi", "lo")}

        rot = {"q": sb("rot_q", [P, 2, H, D]), "k": sb("rot_k", [P, 2, H, D])}
        rot_sin = {"q": sb("sin_q", [P, H, D]), "k": sb("sin_k", [P, H, D])}
        qkT = {"q": sb("qT", [P, 2, PAIRS, P]), "k": sb("kT", [P, 2, PAIRS, P])}
        S = sb("S", [P, 2, PAIRS, C])
        A = [sb(f"A{e}", [P, 2, PAIRS, P]) for e in range(2)]
        Z = [sb(f"Z{e}", [P, 2, PAIRS, P]) for e in range(2)]
        N = sb("N", [P, NN, 2, PAIRS, V])
        gn_stats = sb("gn_stats", [P, 2, H, 6])
        gn_mv = sb("gn_mv", [P, 2, H, 2])
        gn_var = sb("gn_var", [P, 2, H])
        gn_rstd = sb("gn_rstd", [P, 2, H])
        gate = sb("gate", [P, 2, W])
        scaled = sb("scaled", [P, 2, W])
        y = sb("y", [P, 3, W])

        attn = sb("attn", [P, GC, C])
        h2T = sb("h2T", [P, GB, 1 + W])
        delta = sb("delta", [P, W])
        mixed = {"r": sb("mix_r", [P, W]), "k": sb("mix_k", [P, W])}
        k_act = sb("k_act", [P, W])
        r_tanh = sb("r_tanh", [P, GC, C])

        banks = [ctx.enter_context(nc.psum_tensor(f"bank{n}", [P, W], F32)) for n in range(8)]
        state_bank, out_bank = banks[6], banks[7]
        ring = list(range(6))

        pe, act, dve, pool, sp = [], [], [], [], []
        semaphores, count, did, waited = {}, {}, {}, {}

        def promise(done, step=1):
            name, index = done
            if name not in semaphores:
                semaphores[name] = ctx.enter_context(nc.semaphore(name))
                count[name] = 0
            count[name] += step
            assert done not in did
            did[done] = (name, count[name])

        def emit(queue, make, done=None, step=1):
            if done is None:
                queue.append(lambda e: make(e))
            else:
                promise(done, step)
                s = semaphores[done[0]]
                queue.append(lambda e: make(e).then_inc(s, step))

        def wait(queue, name, index=0):
            if index < 0:
                return
            sem, value = did[name, index]
            if waited.get((id(queue), sem), 0) >= value:
                return
            waited[id(queue), sem] = value
            s = semaphores[sem]
            queue.append(lambda e: e.wait_ge(s, value))

        def matmul(o, lhsT, rhs, start, stop, done=None):
            emit(pe, lambda e: e.matmul(o, lhsT, rhs, start=start, stop=stop, skip_group_check=True), done)

        def transpose(o, i, done=None):
            emit(pe, lambda e: e.transpose(o, i, ident), done)

        def activate(o, i, func, done=None, **kw):
            emit(act, lambda e: e.activation(o, i, func, **kw), done)

        def tt(q, o, a, b, op, done=None):
            emit(q, lambda e: e.tensor_tensor(o, a, b, op), done)

        def ts(q, o, a, s1, s2, op0, op1=None, done=None):
            if op1 is None:
                emit(q, lambda e: e.tensor_scalar(o, a, s1, s2, op0), done)
            else:
                emit(q, lambda e: e.tensor_scalar(o, a, s1, s2, op0, op1), done)

        def stt(q, o, a, s, b, op0, op1, done=None):
            emit(q, lambda e: e.scalar_tensor_tensor(out=o, in0=a, scalar=s, in1=b, op0=op0, op1=op1), done)

        def dma(q, o, i, done):
            emit(q, lambda e: e.dma_start(o, i), done, 16)

        last_reader = {}

        def take_bank(freed_by):
            n = ring.pop(0)
            ring.append(n)
            if n in last_reader:
                wait(pe, *last_reader[n])
            last_reader[n] = freed_by
            return banks[n]

        def by(n, ap):
            return ap.rearrange("p (a b) -> p a b", a=n)

        x_rows = x.rearrange("b (g j p) c -> (b g) p j c", j=GC, p=P)
        out_rows = out.rearrange("b (g j p) c -> (b g) p j c", j=GC, p=P)

        def wait_stored(g):
            wait(sp, "out%d" % (g % NX), g // NX)

        def load_x(g):
            wait_stored(g - NX)
            dma(sp, X[:, g % NX, :, :], x_rows[g], ("x%d" % (g % NX), g // NX))

        def wait_x(q, g):
            wait(q, "x%d" % (g % NX), g // NX)

        raw = N[:, :, :, :, :].rearrange("p n e a v -> p (n e a v)")
        raw_qk, raw_g = raw[:, 0:2 * H * D], raw[:, 2 * H * D:2 * H * D + H * V]

        def prologue_loads():
            load_x(0)
            dma(sp, consts[:, :], const, ("const", 0))
            dma(sp, raw_qk, w_qkT, ("w_qk", 0))
            dma(sp, raw_g, w_gT, ("w_g", 0))
            dma(act, cond[:, :], cT, ("cond", 0))
            dma(act, wmod[:, :], w_mod, ("w_mod", 0))
            dma(act, wv[:, :, :].rearrange("p h v -> p (h v)"), w_vT, ("w_v", 0))
            dma(sp, gn[:, :, :], norm_wb, ("gn", 0))
            dma(sp, wo[:, :, :].rearrange("p h v -> p (h v)"), w_oT, ("w_o", 0))
            dma(sp, wffn[:, :, :].rearrange("p h v -> p (h v)"), w_ffnT, ("w_ffn", 0))
            dma(sp, mu[:, :], ffn_mu, ("mu", 0))
            for g in range(1, NX):
                load_x(g)

        def prologue():
            emit(pool, lambda e: e.memset(minus_half[:, :], -0.5))
            emit(pool, lambda e: e.memset(eps[:, :], EPS), ("small_consts", 0))
            emit(pool, lambda e: e.memset(h2T[:, 0, 0:1], 0.0), ("zero_column", 0))
            wait(pool, "small_consts")
            wait(act, "cond")
            activate(silu_c[:, :], cond[:, :], ACT.Silu, ("silu_c", 0))

        def split_weights(name, raw_w, parts):
            wait(act, name)
            activate(parts["hi"][:, :], raw_w, ACT.Copy, (name + "_hi", 0))
            wait(dve, name + "_hi")
            tt(dve, parts["lo"][:, :], raw_w, parts["hi"][:, :].bitcast(F32), ALU.subtract, (name + "_lo", 0))

        def mod_columns():
            bank = take_bank(("mod_cols", 0))
            wait(pe, "silu_c")
            wait(pe, "w_mod")
            for n, k in enumerate((3, 4)):
                matmul(bank[:, n * B:(n + 1) * B], wmod[:, k * C:(k + 1) * C], silu_c[:, :], True, True,
                       ("mod_cols_psum", n))
            wait(dve, "mod_cols_psum", 1)
            ts(dve, mod_cols[:, 0, :], bank[:, 0:B], 0.0, None, ALU.add)
            ts(dve, mod_cols[:, 1, :], bank[:, B:2 * B], 1.0, None, ALU.add, done=("mod_cols", 0))

        def mod_input(b):
            wait(dve, "silu_c")
            wait(dve, "mod_psum", b - 1)
            ts(dve, silu_rows[:, :], silu_c[:, b:b + 1].broadcast_to([P, P]), 0.0, None, ALU.add,
               done=("silu_rows", b))

        def mod_rows(b):
            m = mod[:, b % NMOD, :, :]
            bank = take_bank(("mod_gates_read", b))
            wait(pe, "w_mod")
            wait(pe, "silu_rows", b)
            matmul(bank[:, 0:3 * C], silu_rows[:, :], wmod[:, 0:3 * C], True, True)
            matmul(bank[:, 3 * C:4 * C], silu_rows[:, :], wmod[:, 5 * C:6 * C], True, True, ("mod_psum", b))
            wait(dve, "mod_psum", b)
            wait(dve, "ffn_out", GB * (b - NMOD) + GB - 1)
            wait(dve, "mod_gates", b - 1)
            ts(dve, m[:, 0, :], bank[:, 0:C], 0.0, None, ALU.add)
            ts(dve, m[:, 1, :], bank[:, C:2 * C], 1.0, None, ALU.add, done=("mod_shift", b))
            gates = by(2, bank[:, 2 * C:4 * C])
            ts(dve, mod_pos[:, :, :], gates, 0.25, None, ALU.max, done=("mod_pos", b))
            ts(dve, mod_neg[:, :, :], gates, -0.25, None, ALU.min, done=("mod_neg", b))
            wait(dve, "mod_pos", b)
            stt(dve, mod_pos[:, :, :], gates, 0.0, mod_pos[:, :, :], ALU.is_ge, ALU.mult)
            wait(dve, "mod_neg", b)
            stt(dve, mod_neg[:, :, :], gates, 0.0, mod_neg[:, :, :], ALU.is_lt, ALU.mult, ("mod_gates_read", b))
            wait(dve, "mod_gates_read", b)
            tt(dve, m[:, 2:4, :], mod_pos[:, :, :], mod_neg[:, :, :], ALU.add, ("mod_gates", b))

        def key_tables(c):
            wait(pool, "const")
            for n, table in enumerate((kcos, ksin)):
                tt(pool, table[:, c, :, :], rotary[:, c, n, :].unsqueeze(1).broadcast_to([P, H, D]),
                   key_decay[:, c, :].unsqueeze(2).broadcast_to([P, H, D]), ALU.mult,
                   ("key_tables", c) if n else None)

        def norm_stats(g, which):
            if which == 0:
                wait_x(dve, g)
            else:
                wait(dve, "residual", g)
            wait(dve, f"ln_apply{which}", g - 1)
            for j in range(GC):
                i, o = X[:, g % NX, j, :], ln_stats[:, which, j, :]
                emit(dve, lambda e, i=i, o=o: e.bn_stats(o, i), (f"ln_stats{which}", GC * g + j))
            for j in range(GC):
                wait(dve, f"ln_stats{which}", GC * g + j)
                i, o = ln_stats[:, which, j, :], ln_mv[:, which, j, :]
                emit(dve, lambda e, i=i, o=o: e.bn_aggr(o, i), (f"ln_mv{which}", GC * g + j))
            wait(pool, f"ln_mv{which}", GC * g + GC - 1)
            tt(pool, ln_var[:, which, :], ln_mv[:, which, :, 1], eps[:, :].broadcast_to([P, GC]), ALU.add,
               (f"ln_var{which}", g))
            wait(pool, f"ln_var{which}", g)
            tt(pool, ln_rstd[:, which, :], ln_var[:, which, :], minus_half[:, :].broadcast_to([P, GC]), ALU.pow,
               (f"ln_rstd{which}", g))

        def norm_apply(g, which):
            o = (normed, normed2)[which]
            wait(dve, f"ln_rstd{which}", g)
            wait(dve, ("h_scaled", "n2T")[which], g - 1)
            for j in range(GC):
                ts(dve, o[:, j, :], X[:, g % NX, j, :], ln_mv[:, which, j, 0:1], ln_rstd[:, which, j:j + 1],
                   ALU.subtract, ALU.mult, (f"ln_apply{which}", g) if j == GC - 1 else None)

        def modulate(g):
            m, h = mod[:, (g // GB) % NMOD, :, :], h_nat[:, g % NHN, :, :]
            wait(pool, "ln_apply0", g)
            wait(pool, "mod_shift", g // GB)
            wait(pool, "z_O", GC * (g - NHN) + GC - 1)
            tt(pool, h, normed[:, :, :], m[:, 1:2, :].broadcast_to([P, GC, C]), ALU.mult, ("h_scaled", g))
            wait(pool, "h_scaled", g)
            tt(pool, h, h, m[:, 0:1, :].broadcast_to([P, GC, C]), ALU.add, ("h_nat", g))

        def transpose_h(g):
            bank = take_bank(("hT_lo", g))
            wait(pe, "h_nat", g)
            wait(pe, "const")
            for j in range(GC):
                transpose(bank[:, j * P:(j + 1) * P], h_nat[:, g % NHN, j, :], ("hT_psum", GC * g + j))
            wait(act, "hT_psum", GC * g + GC - 1)
            wait(act, "gate_psum", H * (g - NHT) + H - 1)
            activate(hT["hi"][:, g % NHT, :], bank[:, :], ACT.Copy, ("hT_hi", g))
            wait(dve, "hT_hi", g)
            wait(dve, "gate_psum", H * (g - NHT) + H - 1)
            tt(dve, hT["lo"][:, g % NHT, :], bank[:, :], hT["hi"][:, g % NHT, :].bitcast(F32), ALU.subtract,
               ("hT_lo", g))

        def project(i):
            g, j = divmod(i, GC)
            hi, lo = (hT[s][:, g % NHT, j * P:(j + 1) * P] for s in ("hi", "lo"))
            c = i % CB
            for n, what in enumerate("qk"):
                cols = slice(n * H * D, (n + 1) * H * D)
                bank = take_bank(("sin_" + what, i))
                wait(pe, "w_qk_lo")
                wait(pe, "hT_hi", g)
                wait(pe, "hT_lo", g)
                matmul(bank[:, :], hi, wqk["hi"][:, cols], True, False)
                matmul(bank[:, :], hi, wqk["lo"][:, cols], False, False)
                matmul(bank[:, :], lo, wqk["hi"][:, cols], False, True, ("proj_" + what, i))
                heads = by(H, bank[:, :])
                halves = bank[:, :].rearrange("p (h k d) -> p h k d", h=H, k=2)
                sines = rot_sin[what][:, :, :]
                if what == "q":
                    cos = rotary[:, c, 0:1, :].broadcast_to([P, H, D])
                    sin = rotary[:, c, 1:2, :].broadcast_to([P, H, D])
                else:
                    wait(dve, "key_tables", c)
                    cos, sin = kcos[:, c, :, :], ksin[:, c, :, :]
                turned = rot[what][:, i % 2, :, :]
                wait(dve, "const")
                wait(dve, "proj_" + what, i)
                wait(dve, {"q": "T_q", "k": "state"}[what], i - 2)
                wait(dve, "T_" + what, i - 2)
                tt(dve, turned, heads, cos, ALU.mult, ("cos_" + what, i))
                wait(dve, "rot_" + what, i - 1)
                tt(dve, sines.rearrange("p h (k d) -> p h k d", k=2), halves[:, :, ::-1, :],
                   sin.rearrange("p h (k d) -> p h k d", k=2), ALU.mult, ("sin_" + what, i))
                wait(pool, "cos_" + what, i)
                wait(pool, "sin_" + what, i)
                tt(pool, turned, turned, sines, ALU.add, ("rot_" + what, i))

        def transpose_qk(i):
            for what in "qk":
                bank = take_bank((what + "T", i))
                wait(pe, "rot_" + what, i)
                flat = rot[what][:, i % 2, :, :].rearrange("p h d -> p (h d)")
                for n in range(PAIRS):
                    transpose(bank[:, n * P:(n + 1) * P], flat[:, n * P:(n + 1) * P],
                              ("T_" + what, i) if n == PAIRS - 1 else None)
                wait(act, "T_" + what, i)
                wait(act, "scores_O", i - 2)
                wait(act, "z_O", i - 2)
                activate(qkT[what][:, i % 2, :, :], by(PAIRS, bank[:, :]), ACT.Copy, done=(what + "T", i))

        def accumulate_state(i):
            g, j = divmod(i, GC)
            if i % CB == CB - 1:
                did["state", i] = did["state", i - 1]
                return
            wait(pe, "S", i - 1 if i % CB else i - 2)
            wait(pe, "rot_k", i)
            wait(pe, "h_nat", g)
            flat = rot["k"][:, i % 2, :, :].rearrange("p h d -> p (h d)")
            for n in range(PAIRS):
                matmul(state_bank[:, n * C:(n + 1) * C], flat[:, n * P:(n + 1) * P], h_nat[:, g % NHN, j, :],
                       i % CB == 0 and n == 0, True, ("state", i) if n == PAIRS - 1 else None)
            wait(act, "state", i)
            wait(act, "z_O", i - 1)
            activate(S[:, i % 2, :, :], by(PAIRS, state_bank[:, :]), ACT.Copy, done=("S", i))

        def scores(i):
            s = i % 2
            e_bank, o_bank = take_bank(("A_E", i)), take_bank(("A_O", i))
            wait(pe, "qT", i)
            wait(pe, "kT", i)
            for n in range(PAIRS):
                for odd, bank in enumerate((e_bank, o_bank)):
                    rows = slice(odd * D, (odd + 1) * D)
                    matmul(bank[:, n * P:(n + 1) * P], qkT["k"][rows, s, n, :], qkT["q"][rows, s, n, :], True, True,
                           ("scores_" + "EO"[odd], i) if n == PAIRS - 1 else None)
            for odd, bank in enumerate((e_bank, o_bank)):
                wait(dve, "scores_" + "EO"[odd], i)
                wait(dve, "z_O", i - 2)
                tt(dve, A[odd][:, s, :, :], by(PAIRS, bank[:, :]), causal.unsqueeze(1).broadcast_to([P, PAIRS, P]),
                   ALU.mult, ("A_" + "EO"[odd], i))

        def mix_tokens(i):
            g, j = divmod(i, GC)
            s, first = i % 2, i % CB == 0
            pair = take_bank(("Z_E", i)), take_bank(("Z_O", i))
            for odd, bank in enumerate(pair):
                wait(pe, "A_" + "EO"[odd], i)
                matmul(bank[:, :], h_nat[:, g % NHN, j, :], A[odd][:, s, :, :].rearrange("p a t -> p (a t)"),
                       True, first, ("z_" + "EO"[odd], i) if first else None)
            if not first:
                wait(pe, "S", i - 1)
                for n in range(PAIRS):
                    for odd, bank in enumerate(pair):
                        rows = slice(odd * D, (odd + 1) * D)
                        matmul(bank[:, n * P:(n + 1) * P], S[rows, (i - 1) % 2, n, :], qkT["q"][rows, s, n, :],
                               False, n == PAIRS - 1, ("z_" + "EO"[odd], i) if n == PAIRS - 1 else None)
            for odd, bank in enumerate(pair):
                wait(act, "z_" + "EO"[odd], i)
                wait(act, "heads_O", i - 2)
                activate(Z[odd][:, s, :, :], by(PAIRS, bank[:, :]), ACT.Copy, done=("Z_" + "EO"[odd], i))

        def head_outputs(i):
            s, slot, c = i % 2, i % NN, i % CB
            for odd in range(2):
                eo = "EO"[odd]
                bank = take_bank(("O_" + eo, i))
                wait(pe, "Z_" + eo, i)
                wait(pe, "w_v")
                for n in range(PAIRS):
                    matmul(bank[:, n * V:(n + 1) * V], Z[odd][:, s, n, :], wv[:, 2 * n + odd, :], True, True,
                           ("heads_" + eo, i) if n == PAIRS - 1 else None)
                wait(act, "heads_" + eo, i)
                wait(act, "nT_psum", H * ((i - NN) // GC) + H - 1)
                wait(act, "w_g_lo")
                wait(act, "w_qk_lo")
                activate(N[:, slot, odd, :, :], by(PAIRS, bank[:, :]), ACT.Copy, done=("O_" + eo, i))
            wait(dve, "gn_apply", i - 2)
            for odd in range(2):
                wait(dve, "O_" + "EO"[odd], i)
                for n in range(PAIRS):
                    k = odd * PAIRS + n
                    a, o = N[:, slot, odd, n, :], gn_stats[:, s, k, :]
                    emit(dve, lambda e, a=a, o=o: e.bn_stats(o, a), ("gn_stats", H * i + k))
            for k in range(H):
                wait(dve, "gn_stats", H * i + k)
                a, o = gn_stats[:, s, k, :], gn_mv[:, s, k, :]
                emit(dve, lambda e, a=a, o=o: e.bn_aggr(o, a), ("gn_mv", i) if k == H - 1 else None)
            wait(pool, "gn_mv", i)
            wait(pool, "gn_apply", i - 2)
            eps_eo = norm_eps[:, c, :].rearrange("p (a e) -> p e a", e=2)
            tt(pool, by(2, gn_var[:, s, :]), gn_mv[:, s, :, 1].rearrange("p (e a) -> p e a", e=2), eps_eo, ALU.add,
               ("gn_var", i))
            wait(pool, "gn_var", i)
            tt(pool, gn_rstd[:, s, :], gn_var[:, s, :], minus_half[:, :].broadcast_to([P, H]), ALU.pow,
               ("gn_rstd", i))

        def norm_heads(i):
            s, slot = i % 2, i % NN
            wait(dve, "gn_rstd", i)
            for k in range(H):
                a = N[:, slot, k // PAIRS, k % PAIRS, :]
                ts(dve, a, a, gn_mv[:, s, k, 0:1], gn_rstd[:, s, k:k + 1], ALU.subtract, ALU.mult,
                   ("gn_apply", i) if k == H - 1 else None)

        def gate_head(g, h):
            n = H * g + h
            cols = slice(h * V, (h + 1) * V)
            hi, lo = (hT[s][:, g % NHT, :] for s in ("hi", "lo"))
            bank = take_bank(("gate", n))
            wait(pe, "w_g_lo")
            matmul(bank[:, :], wg["hi"][:, cols], hi, True, False)
            matmul(bank[:, :], wg["hi"][:, cols], lo, False, False)
            matmul(bank[:, :], wg["lo"][:, cols], hi, False, True, ("gate_psum", n))
            wait(act, "gate_psum", n)
            wait(act, "y", n - 2)
            activate(gate[:, n % 2, :], bank[:, :], ACT.Silu, ("gate", n))
            bank = take_bank(("scaled", n))
            wait(pe, "gn_apply", GC * g + GC - 1)
            for j in range(GC):
                transpose(bank[:, j * P:(j + 1) * P], N[:, (GC * g + j) % NN, h % 2, h // 2, :],
                          ("nT_psum", n) if j == GC - 1 else None)
            wait(act, "nT_psum", n)
            wait(act, "gn")
            activate(scaled[:, n % 2, :], bank[:, :], ACT.Identity, ("scaled", n), bias=gn[:, 1, h:h + 1],
                     scale=gn[:, 0, h:h + 1])
            wait(pool, "gate", n)
            wait(pool, "scaled", n)
            wait(pool, "out_head", n - 3)
            tt(pool, y[:, n % 3, :], scaled[:, n % 2, :], gate[:, n % 2, :], ALU.mult, ("y", n))

        def project_out(g, h):
            n = H * g + h
            wait(pe, "w_o")
            wait(pe, "y", n)
            if h == 0:
                wait(pe, "attn", g - 1)
            for j in range(GC):
                matmul(out_bank[:, j * C:(j + 1) * C], y[:, n % 3, j * P:(j + 1) * P], wo[:, h, :],
                       h == 0 and j == 0, h == H - 1, ("out_head", n) if j == GC - 1 else None)

        def residual(g):
            m = mod[:, (g // GB) % NMOD, :, :]
            xg = X[:, g % NX, :, :]
            wait(dve, "out_head", H * g + H - 1)
            wait(dve, "ffn_out", g - 1)
            wait(dve, "mod_gates", g // GB)
            tt(dve, attn[:, :, :], by(GC, out_bank[:, :]), m[:, 2:3, :].broadcast_to([P, GC, C]), ALU.mult,
               ("attn", g))
            wait(pool, "attn", g)
            tt(pool, xg, xg, attn[:, :, :], ALU.add, ("residual", g))

        def transpose_n2(g):
            b, half = divmod(g, GB)
            bank = take_bank(("h2T", g))
            wait(pe, "ln_apply1", g)
            for j in range(GC):
                transpose(bank[:, j * P:(j + 1) * P], normed2[:, j, :], ("n2T", g) if j == GC - 1 else None)
            wait(act, "n2T", g)
            wait(act, "mod_cols")
            wait(act, "mix_k", g - 2)
            wait(act, "h2T_edge", g - 1 if half == 0 else -1)
            activate(h2T[:, half, 1:1 + W], bank[:, :], ACT.Identity, ("h2T", g), bias=mod_cols[:, 0, b:b + 1],
                     scale=mod_cols[:, 1, b:b + 1])
            if half:
                wait(act, "h2T", g - 1)
                activate(h2T[:, half, 0:1], h2T[:, half - 1, W:W + 1], ACT.Copy, ("h2T_edge", g))

        def mix_shift(g):
            half = g % GB
            now, before = h2T[:, half, 1:1 + W], h2T[:, half, 0:W]
            for q in (pool, dve):
                wait(q, "h2T", g)
                if half:
                    wait(q, "h2T_edge", g)
                else:
                    wait(q, "zero_column")
            wait(pool, "mix_k", g - 1)
            tt(pool, delta[:, :], now, before, ALU.subtract, ("delta", g))
            wait(dve, "delta", g)
            wait(dve, "mu")
            wait(dve, "rk_psum", 2 * (g - 1) + 1)
            for n, what in enumerate("rk"):
                stt(dve, mixed[what][:, :], delta[:, :], mu[:, n:n + 1], before, ALU.mult, ALU.add,
                    ("mix_" + what, g))

        def ffn_in(g):
            bank = take_bank(("r_tanh", g))
            wait(pe, "w_ffn")
            wait(pe, "mix_r", g)
            for j in range(GC):
                matmul(bank[:, j * C:(j + 1) * C], mixed["r"][:, j * P:(j + 1) * P], wffn[:, 0, :], True, True,
                       ("rk_psum", 2 * g) if j == GC - 1 else None)
            wait(act, "rk_psum", 2 * g)
            wait(act, "ffn_product", g - 1)
            activate(r_tanh[:, :, :], by(GC, bank[:, :]), ACT.Tanh, ("r_tanh", g), scale=0.5)
            bank = take_bank(("relu", g))
            wait(pe, "mix_k", g)
            matmul(bank[:, :], wffn[:, 1, :], mixed["k"][:, :], True, True, ("rk_psum", 2 * g + 1))
            wait(act, "rk_psum", 2 * g + 1)
            wait(act, "ffn_psum", g - 1)
            activate(k_act[:, :], bank[:, :], ACT.Relu, ("relu", g))
            wait(act, "relu", g)
            activate(k_act[:, :], k_act[:, :], ACT.Square, ("k_act", g))

        def ffn_gate(g):
            m = mod[:, (g // GB) % NMOD, :, :]
            wait(dve, "r_tanh", g)
            stt(dve, r_tanh[:, :, :], r_tanh[:, :, :], 1.0, m[:, 3:4, :].broadcast_to([P, GC, C]), ALU.add, ALU.mult,
                ("r_gate", g))

        def ffn_out(g):
            xg = X[:, g % NX, :, :]
            bank = take_bank(("ffn_product", g))
            wait(pe, "k_act", g)
            for j in range(GC):
                matmul(bank[:, j * C:(j + 1) * C], k_act[:, j * P:(j + 1) * P], wffn[:, 2, :], True, True,
                       ("ffn_psum", g) if j == GC - 1 else None)
            wait(dve, "ffn_psum", g)
            wait(dve, "r_gate", g)
            wait(dve, "residual", g)
            wait(dve, "ffn_out", g - 1)
            stt(dve, attn[:, :, :], by(GC, bank[:, :]), 0.5, r_tanh[:, :, :], ALU.mult, ALU.mult, ("ffn_product", g))
            wait(pool, "ffn_product", g)
            tt(pool, xg, xg, attn[:, :, :], ALU.add, ("ffn_out", g))
            wait(sp, "ffn_out", g)
            dma(sp, out_rows[g], xg, ("out%d" % (g % NX), g // NX))

        prologue_loads()
        prologue()
        norm_stats(0, 0)
        mod_input(0)
        mod_rows(0)
        norm_apply(0, 0)
        modulate(0)
        key_tables(0)
        split_weights("w_qk", raw_qk, wqk)
        transpose_h(0)
        mod_columns()
        project(0)
        split_weights("w_g", raw_g, wg)
        norm_stats(1, 0)

        last_step = NCHUNK + 3 * GC + 2
        for step in range(last_step):
            i = step
            done_i = step - 1
            gg, gj = divmod(step - GC - 1, GC)
            g_now, j_now = divmod(step, GC)
            if i + 1 < NCHUNK:
                if i + 1 < CB:
                    key_tables(i + 1)
                project(i + 1)
            if j_now == 2 and g_now + 1 < NGROUP:
                transpose_h(g_now + 1)
            if 0 <= done_i < NCHUNK:
                mix_tokens(done_i)
            if 0 <= gg < NGROUP:
                gate_head(gg, 2 * gj)
            if gj == 0 and 0 <= gg - 2 < NGROUP:
                ffn_out(gg - 2)
                if gg - 2 + NX < NGROUP:
                    load_x(gg - 2 + NX)
            if gj and 0 <= gg < NGROUP:
                project_out(gg, 2 * gj - 1)
            if gj == 0 and 0 < gg <= NGROUP:
                project_out(gg - 1, H - 1)
                residual(gg - 1)
            if i < NCHUNK:
                transpose_qk(i)
            if 0 <= done_i < NCHUNK:
                head_outputs(done_i)
            if i < NCHUNK:
                accumulate_state(i)
                scores(i)
            if 0 <= done_i < NCHUNK:
                norm_heads(done_i)
            if 0 <= gg < NGROUP:
                gate_head(gg, 2 * gj + 1)
                project_out(gg, 2 * gj)
            done = gg - 1
            if 0 <= done < NGROUP:
                if gj == 0:
                    norm_stats(done, 1)
                if gj == 1:
                    norm_apply(done, 1)
                if gj == 2:
                    transpose_n2(done)
                    mix_shift(done)
                if gj == 3:
                    ffn_in(done)
                    ffn_gate(done)
            nxt = g_now + 1
            if j_now == 0 and nxt < NGROUP:
                norm_apply(nxt, 0)
                modulate(nxt)
            if j_now == 2 and (nxt + 1) % GB == 0 and nxt + 1 < NGROUP:
                mod_input((nxt + 1) // GB)
            if j_now == 3 and nxt + 1 < NGROUP:
                if (nxt + 1) % GB == 0:
                    mod_rows((nxt + 1) // GB)
                norm_stats(nxt + 1, 0)
        for g in range(max(0, NGROUP - NX), NGROUP):
            wait_stored(g)

        block = ctx.enter_context(nc.Block())

        @block.tensor
        def _(e):
            for f in pe:
                f(e)

        @block.scalar
        def _(e):
            for f in act:
                f(e)

        @block.vector
        def _(e):
            for f in dve:
                f(e)

        @block.gpsimd
        def _(e):
            for f in pool:
                f(e)

        @block.sync
        def _(e):
            for f in sp:
                f(e)


def kernel(L0_attn_x, L0_attn_Wq, L0_attn_Wk, L0_attn_Wv, L0_attn_Wg, L0_attn_Wo, L0_attn_gn_weight,
           L0_attn_gn_bias, L0_ffn_W_r, L0_ffn_W_k, L0_ffn_W_v, L0_ffn_mu_r, L0_ffn_mu_k, L0_c, L0_wmod):
    import concourse.bacc as bacc
    from concourse.bass_utils import run_bass_kernel_spmd

    def a(v):
        return np.asarray(v)

    lay = np.ascontiguousarray
    arrays = {
        "x": lay(a(L0_attn_x)),
        "cT": lay(a(L0_c).T),
        "w_mod": lay(a(L0_wmod)),
        "w_qkT": lay(np.concatenate([a(L0_attn_Wq), a(L0_attn_Wk)], 0).T),
        "w_gT": lay(a(L0_attn_Wg).T),
        "w_vT": lay(a(L0_attn_Wv).T),
        "w_oT": lay(a(L0_attn_Wo).T.reshape(H, V, C).transpose(1, 0, 2).reshape(V, H * C)),
        "norm_wb": lay(np.stack([a(L0_attn_gn_weight), a(L0_attn_gn_bias)]).reshape(2, H, V).transpose(2, 0, 1)),
        "w_ffnT": lay(np.concatenate([a(L0_ffn_W_r).T, a(L0_ffn_W_k).T, a(L0_ffn_W_v).T], 1)),
        "ffn_mu": lay(np.stack([a(L0_ffn_mu_r), a(L0_ffn_mu_k)], 1)),
        "const": constants(),
    }
    nc = bacc.Bacc("TRN2", target_bir_lowering=False, num_devices=1)
    ins = [nc.dram_tensor("in_" + n, v.shape, mybir.dt.from_np(v.dtype), kind="ExternalInput").ap()
           for n, v in arrays.items()]
    out = nc.dram_tensor("out", (B, T, C), F32, kind="ExternalOutput").ap()
    build(nc, *ins, out)
    r = run_bass_kernel_spmd(nc, [{"in_" + n: v for n, v in arrays.items()}], core_ids=[0])
    return r.results[0]["out"]
```

```python
from contextlib import ExitStack

import numpy as np

import concourse.bass as bass
from concourse import mybir

F32 = mybir.dt.float32
F32R = mybir.dt.float32r
ALU = mybir.AluOpType
ACT = mybir.ActivationFunctionType

P = 128
B, T, C = 8, 1024, 128
H, D, V = 8, 64, 128
PAIRS = H // 2
QUARTER = D // 4
GC = 4
NCHUNK = B * T // P
NGROUP = NCHUNK // GC
CB = T // P
GB = CB // GC
W = GC * P
EPS = 1e-5
MID = T // 2
UC = 2
UW = UC * P

NX, NHT, NHN, NMOD, NN = 5, 3, 2, 3, 2 * GC
NKT, NSPLIT, NGN, NSWAP = 1, 1, 2, 1

PROLOGUE = ["mod_input", "key_tables", "norm_stats0", "norm_apply0", "mod_rows", "modulate", "split_w_qk",
    "transpose_h", "split_hT", "project_k", "project_q_0", "project_q_1", "rotate_k", "rotate_q_0", "split_w_g",
    "rotate_q_1", "mod_columns"]
ORDER = [("key_tables", -1), ("modulate", -3), ("act_k", 13), ("rotate_q_0", -1), ("ffn_gate", 13),
    ("transpose_k", 0), ("mix_shift", 12), ("project_ffn_out", 13), ("gate_silu_0", 5), ("turn_head_0", 5),
    ("scale_head_0", 5), ("ffn_out", 13), ("norm_stats1", 10), ("norm_apply1", 11), ("load_x", 15), ("mix", 1),
    ("transpose_h", -2), ("project_k", -1), ("project_out_1", 6), ("gate_head_0", 5), ("copy_kT", 0),
    ("rotate_k", -1), ("copy_Z", 1), ("split_h", 0), ("project_q_1", -1), ("head_outputs_O", 1),
    ("residual", 9), ("split_hT", -2), ("copy_state", 0), ("scores", 0), ("copy_outputs_O", 1),
    ("rotate_q_1", -1), ("transpose_n2", 11), ("head_outputs_E", 1), ("norm_stats0", -4), ("modulate2", 11),
    ("project_r", 12), ("head_stats_O", 1), ("turn_head_1", 5), ("project_gate_1", 5), ("copy_outputs_E", 1),
    ("scale_head_1", 5), ("mask_E", 0), ("mask_O", 0), ("head_stats_E", 1), ("mod_input", -6), ("act_r", 12),
    ("project_ffn_k", 12), ("norm_apply0", -4), ("split_E", 0), ("project_gate_0", 4), ("split_O", 0),
    ("mod_rows", -5), ("project_out_0", 5), ("head_rstd", 1), ("gate_silu_1", 5), ("state", -1),
    ("gate_head_1", 5), ("project_q_0", -2), ("norm_heads", 1)]


PARTNERS = [(n + QUARTER) % (2 * QUARTER) for n in range(2 * QUARTER)]


def constants():
    inv_freq = (np.float32(1.0) / np.float32(10000.0) ** (np.arange(0, D, 2, dtype=np.float32) / np.float32(D)))
    angle = (np.arange(T, dtype=np.float32)[:, None] * inv_freq.astype(np.float32)[None, :]).astype(np.float32)
    cos, sin = np.cos(angle), np.sin(angle)
    tables = np.stack([np.concatenate([cos, cos], 1), np.concatenate([-sin, sin], 1)])
    tables = tables.reshape(2, T, 2, 2, QUARTER).transpose(0, 1, 3, 2, 4).reshape(2, T, D)
    rotary = tables.transpose(1, 0, 2)
    rotary_q = np.concatenate([tables, tables], 2).transpose(2, 0, 1).reshape(P, 2 * T)
    gamma = 1.0 - np.exp2(-5.0 - np.arange(H, dtype=np.float64))
    away = MID - np.arange(T, dtype=np.float64)
    key_decay = gamma[None, :] ** away[:, None]
    norm_eps = EPS * D * key_decay ** 2
    causal = (np.arange(P)[:, None] <= np.arange(P)[None, :])
    by_partition = lambda a: a.reshape(CB, P, -1).transpose(1, 0, 2).reshape(P, -1)
    parts = [by_partition(rotary), by_partition(key_decay), by_partition(norm_eps), causal, np.eye(P), rotary_q]
    return np.ascontiguousarray(np.concatenate(parts, 1).astype(np.float32))


def build(nc, x, cT, w_mod, w_qkT, w_gT, w_vT, w_oT, norm_wb, w_ffnT, ffn_mu, const, out):
    with ExitStack() as ctx:
        def sb(name, shape, dt=F32):
            return ctx.enter_context(nc.sbuf_tensor(name, shape, dt))

        def by(n, ap):
            return ap.rearrange("p (a b) -> p a b", a=n)

        n_const = const.shape[1]
        consts = sb("consts", [P, n_const])
        at = [0]

        def const_part(n):
            at[0] += n
            return consts[:, at[0] - n:at[0]]

        rotary = const_part(CB * 2 * D).rearrange("p (c k d) -> p c k d", c=CB, k=2)
        key_decay = const_part(CB * H).rearrange("p (c h) -> p c h", c=CB)
        norm_eps = const_part(CB * H).rearrange("p (c h) -> p c h", c=CB)
        causal = const_part(P)
        ident = const_part(P)
        rotary_q = const_part(2 * T).rearrange("p (k t) -> p k t", k=2)

        X = sb("X", [P, NX, GC, C])
        kcos = sb("kcos", [P, CB, H, D])
        ksin = sb("ksin", [P, CB, H, D])
        wqk = {s: sb("wqk_" + s, [P, 2 * H * D], F32R) for s in ("hi", "lo")}
        wg = {s: sb("wg_" + s, [P, H * V], F32R) for s in ("hi", "lo")}
        wv = sb("wv", [P, H, V])
        wo = sb("wo", [P, H, C])
        wffn = sb("wffn", [P, 3, C])
        mu = sb("mu", [P, 2])
        gn = sb("gn", [P, 2, H])
        wmod = sb("wmod", [P, 6 * C])
        cond = sb("cond", [P, B])
        silu_c = sb("silu_c", [P, B])
        silu_rows = sb("silu_rows", [P, P])
        mod = sb("mod", [P, NMOD, 4, C])
        mod_pos = sb("mod_pos", [P, 2, C])
        mod_neg = sb("mod_neg", [P, 2, C])
        mod_cols = sb("mod_cols", [P, 2, B])
        minus_half = sb("minus_half", [P, 1])
        eps = sb("eps", [P, 1])

        ln_stats = sb("ln_stats", [P, 2, GC, 6])
        ln_mv = sb("ln_mv", [P, 2, GC, 2])
        ln_var = sb("ln_var", [P, 2, GC])
        ln_rstd = sb("ln_rstd", [P, 2, GC])
        normed = sb("normed", [P, GC, C])
        h_nat = sb("h_nat", [P, NHN, GC, C])
        hT = {s: sb("hT_" + s, [P, NHT, W], F32R) for s in ("hi", "lo")}

        rot_k = sb("rot_k", [P, 2, H, D])
        sin_k = sb("sin_k", [P, H, D])
        kT = sb("kT", [P, NKT, PAIRS, P])
        swapped = sb("swapped", [P, NSWAP, 2, UW])
        qT = sb("qT", [P, 2, PAIRS, UW])
        S = sb("S", [P, 2, PAIRS, C])
        h_split = {s: sb("h_" + s, [P, NSPLIT, C], F32R) for s in ("hi", "lo")}
        A = [sb(f"A{e}", [P, PAIRS, P]) for e in range(2)]
        A_split = {s: [sb(f"A{e}_{s}", [P, NSPLIT, W], F32R) for e in range(2)] for s in ("hi", "lo")}
        Z = [sb(f"Z{e}", [P, PAIRS, P]) for e in range(2)]
        N = sb("N", [P, NN, 2, PAIRS, V])
        gn_stats = sb("gn_stats", [P, NGN, H, 6])
        gn_mv = sb("gn_mv", [P, NGN, H, 2])
        gn_var = sb("gn_var", [P, NGN, H])
        gn_rstd = sb("gn_rstd", [P, NGN, H])
        gate = sb("gate", [P, 2, W])
        scaled = sb("scaled", [P, 2, W])
        y = sb("y", [P, 2, W])

        attn = sb("attn", [P, GC, C])
        h2T = sb("h2T", [P, GB, 1 + W])
        delta = attn[:, :, :].rearrange("p a b -> p (a b)")
        mixed = {"r": sb("mix_r", [P, W]), "k": sb("mix_k", [P, W])}
        k_act = sb("k_act", [P, W])
        r_tanh = by(GC, mixed["r"][:, :])

        banks = [ctx.enter_context(nc.psum_tensor(f"bank{n}", [P, W], F32)) for n in range(8)]
        state_bank, out_bank = banks[6], banks[7]
        ring = list(range(6))

        pe, act, dve, pool, sp = [], [], [], [], []
        semaphores, count, did, waited, latest = {}, {}, {}, {}, {}

        def promise(done, step=1):
            name, index = done
            if name not in semaphores:
                semaphores[name] = ctx.enter_context(nc.semaphore(name))
                count[name] = 0
            count[name] += step
            assert index > latest.get(name, -1)
            latest[name] = index
            did[done] = (name, count[name])

        def emit(queue, make, done=None, step=1):
            if done is None:
                queue.append(lambda e: make(e))
            else:
                promise(done, step)
                s = semaphores[done[0]]
                queue.append(lambda e: make(e).then_inc(s, step))

        def wait(queue, name, index=0):
            if index < 0:
                return
            sem, value = did[name, index]
            if waited.get((id(queue), sem), 0) >= value:
                return
            waited[id(queue), sem] = value
            s = semaphores[sem]
            queue.append(lambda e: e.wait_ge(s, value))

        def matmul(o, lhsT, rhs, start, stop, done=None):
            emit(pe, lambda e: e.matmul(o, lhsT, rhs, start=start, stop=stop, skip_group_check=True), done)

        def transpose(o, i, done=None):
            emit(pe, lambda e: e.transpose(o, i, ident), done)

        def activate(o, i, func, done=None, **kw):
            emit(act, lambda e: e.activation(o, i, func, **kw), done)

        def tt(q, o, a, b, op, done=None):
            emit(q, lambda e: e.tensor_tensor(o, a, b, op), done)

        def ts(q, o, a, s1, s2, op0, op1=None, done=None):
            if op1 is None:
                emit(q, lambda e: e.tensor_scalar(o, a, s1, s2, op0), done)
            else:
                emit(q, lambda e: e.tensor_scalar(o, a, s1, s2, op0, op1), done)

        def stt(q, o, a, s, b, op0, op1, done=None):
            emit(q, lambda e: e.scalar_tensor_tensor(out=o, in0=a, scalar=s, in1=b, op0=op0, op1=op1), done)

        def dma(q, o, i, done):
            emit(q, lambda e: e.dma_start(o, i), done, 16)

        psum = {}
        last_reader = {}

        def take_bank(freed_by):
            n = ring.pop(0)
            ring.append(n)
            if n in last_reader:
                wait(pe, *last_reader[n])
            last_reader[n] = freed_by
            return banks[n]

        x_rows = x.rearrange("b (g j p) c -> (b g) p j c", j=GC, p=P)
        out_rows = out.rearrange("b (g j p) c -> (b g) p j c", j=GC, p=P)

        def wait_stored(g):
            wait(sp, "out%d" % (g % NX), g // NX)

        def load_x(g):
            wait_stored(g - NX)
            dma(sp, X[:, g % NX, :, :], x_rows[g], ("x%d" % (g % NX), g // NX))

        def wait_x(q, g):
            wait(q, "x%d" % (g % NX), g // NX)

        raw = N[:, :, :, :, :].rearrange("p n e a v -> p (n e a v)")
        raw_qk, raw_g = raw[:, 0:2 * H * D], raw[:, 2 * H * D:2 * H * D + H * V]

        def prologue_loads():
            load_x(0)
            dma(sp, consts[:, :], const, ("const", 0))
            dma(sp, raw_qk, w_qkT, ("w_qk", 0))
            dma(sp, raw_g, w_gT, ("w_g", 0))
            dma(act, cond[:, :], cT, ("cond", 0))
            dma(act, wmod[:, :], w_mod, ("w_mod", 0))
            dma(act, wv[:, :, :].rearrange("p h v -> p (h v)"), w_vT, ("w_v", 0))
            dma(sp, gn[:, :, :], norm_wb, ("gn", 0))
            dma(sp, wo[:, :, :].rearrange("p h v -> p (h v)"), w_oT, ("w_o", 0))
            dma(sp, wffn[:, :, :].rearrange("p h v -> p (h v)"), w_ffnT, ("w_ffn", 0))
            dma(sp, mu[:, :], ffn_mu, ("mu", 0))
            for g in range(1, NX):
                load_x(g)

        def prologue():
            emit(pool, lambda e: e.memset(minus_half[:, :], -0.5))
            emit(pool, lambda e: e.memset(eps[:, :], EPS), ("small_consts", 0))
            emit(pool, lambda e: e.memset(h2T[:, 0, 0:1], 0.0), ("zero_column", 0))
            wait(pool, "small_consts")
            wait(act, "cond")
            activate(silu_c[:, :], cond[:, :], ACT.Silu, ("silu_c", 0))

        def split_weights(name, raw_w, parts):
            wait(act, name)
            activate(parts["hi"][:, :], raw_w, ACT.Copy, (name + "_hi", 0))
            wait(dve, name + "_hi")
            tt(dve, parts["lo"][:, :], raw_w, parts["hi"][:, :].bitcast(F32), ALU.subtract, (name + "_lo", 0))

        def mod_columns():
            bank = take_bank(("mod_cols", 0))
            wait(pe, "silu_c")
            wait(pe, "w_mod")
            for n, k in enumerate((3, 4)):
                matmul(bank[:, n * B:(n + 1) * B], wmod[:, k * C:(k + 1) * C], silu_c[:, :], True, True,
                       ("mod_cols_psum", n))
            wait(dve, "mod_cols_psum", 1)
            ts(dve, mod_cols[:, 0, :], bank[:, 0:B], 0.0, None, ALU.add)
            ts(dve, mod_cols[:, 1, :], bank[:, B:2 * B], 1.0, None, ALU.add, done=("mod_cols", 0))

        def mod_input(b):
            wait(dve, "silu_c")
            wait(dve, "mod_psum", b - 1)
            ts(dve, silu_rows[:, :], silu_c[:, b:b + 1].broadcast_to([P, P]), 0.0, None, ALU.add,
               done=("silu_rows", b))

        def mod_rows(b):
            m = mod[:, b % NMOD, :, :]
            bank = take_bank(("mod_gates_read", b))
            wait(pe, "w_mod")
            wait(pe, "silu_rows", b)
            matmul(bank[:, 0:3 * C], silu_rows[:, :], wmod[:, 0:3 * C], True, True)
            matmul(bank[:, 3 * C:4 * C], silu_rows[:, :], wmod[:, 5 * C:6 * C], True, True, ("mod_psum", b))
            wait(dve, "mod_psum", b)
            wait(dve, "ffn_out", GB * (b - NMOD) + GB - 1)
            wait(dve, "mod_gates", b - 1)
            ts(dve, m[:, 0, :], bank[:, 0:C], 0.0, None, ALU.add)
            ts(dve, m[:, 1, :], bank[:, C:2 * C], 1.0, None, ALU.add, done=("mod_shift", b))
            gates = by(2, bank[:, 2 * C:4 * C])
            ts(dve, mod_pos[:, :, :], gates, 0.25, None, ALU.max, done=("mod_pos", b))
            ts(dve, mod_neg[:, :, :], gates, -0.25, None, ALU.min, done=("mod_neg", b))
            wait(dve, "mod_pos", b)
            stt(dve, mod_pos[:, :, :], gates, 0.0, mod_pos[:, :, :], ALU.is_ge, ALU.mult)
            wait(dve, "mod_neg", b)
            stt(dve, mod_neg[:, :, :], gates, 0.0, mod_neg[:, :, :], ALU.is_lt, ALU.mult, ("mod_gates_read", b))
            wait(dve, "mod_gates_read", b)
            tt(dve, m[:, 2:4, :], mod_pos[:, :, :], mod_neg[:, :, :], ALU.add, ("mod_gates", b))

        def key_tables(c):
            wait(pool, "const")
            for n, table in enumerate((kcos, ksin)):
                tt(pool, table[:, c, :, :], rotary[:, c, n, :].unsqueeze(1).broadcast_to([P, H, D]),
                   key_decay[:, c, :].unsqueeze(2).broadcast_to([P, H, D]), ALU.mult,
                   ("key_tables", c) if n else None)

        def norm_stats(g, which):
            if which == 0:
                wait_x(dve, g)
            else:
                wait(dve, "residual", g)
            wait(dve, f"ln_apply{which}", g - 1)
            for j in range(GC):
                i, o = X[:, g % NX, j, :], ln_stats[:, which, j, :]
                emit(dve, lambda e, i=i, o=o: e.bn_stats(o, i), (f"ln_stats{which}", GC * g + j))
            for j in range(GC):
                wait(dve, f"ln_stats{which}", GC * g + j)
                i, o = ln_stats[:, which, j, :], ln_mv[:, which, j, :]
                emit(dve, lambda e, i=i, o=o: e.bn_aggr(o, i), (f"ln_mv{which}", GC * g + j))
            wait(pool, f"ln_mv{which}", GC * g + GC - 1)
            tt(pool, ln_var[:, which, :], ln_mv[:, which, :, 1], eps[:, :].broadcast_to([P, GC]), ALU.add,
               (f"ln_var{which}", g))
            wait(pool, f"ln_var{which}", g)
            tt(pool, ln_rstd[:, which, :], ln_var[:, which, :], minus_half[:, :].broadcast_to([P, GC]), ALU.pow,
               (f"ln_rstd{which}", g))

        normed_users = []

        def norm_apply(g, which):
            wait(dve, f"ln_rstd{which}", g)
            if normed_users:
                wait(dve, *normed_users[-1])
            normed_users.append((("h_scaled", "n2T")[which], g))
            for j in range(GC):
                ts(dve, normed[:, j, :], X[:, g % NX, j, :], ln_mv[:, which, j, 0:1], ln_rstd[:, which, j:j + 1],
                   ALU.subtract, ALU.mult, (f"ln_apply{which}", g) if j == GC - 1 else None)

        def modulate(g):
            m, h = mod[:, (g // GB) % NMOD, :, :], h_nat[:, g % NHN, :, :]
            wait(pool, "ln_apply0", g)
            wait(pool, "mod_shift", g // GB)
            for used in ("z_O", "state", "hT_psum"):
                wait(pool, used, GC * (g - NHN) + GC - 1)
            tt(pool, h, normed[:, :, :], m[:, 1:2, :].broadcast_to([P, GC, C]), ALU.mult, ("h_scaled", g))
            wait(pool, "h_scaled", g)
            tt(pool, h, h, m[:, 0:1, :].broadcast_to([P, GC, C]), ALU.add, ("h_nat", g))

        def transpose_h(g):
            bank = take_bank(("hT_lo", g))
            wait(pe, "h_nat", g)
            wait(pe, "const")
            for j in range(GC):
                transpose(bank[:, j * P:(j + 1) * P], h_nat[:, g % NHN, j, :], ("hT_psum", GC * g + j))
            psum["hT", g] = bank

        def split_hT(g):
            bank = psum.pop(("hT", g))
            wait(act, "hT_psum", GC * g + GC - 1)
            wait(act, "gate_psum", H * (g - NHT) + H - 1)
            activate(hT["hi"][:, g % NHT, :], bank[:, :], ACT.Copy, ("hT_hi", g))
            wait(dve, "hT_hi", g)
            wait(dve, "gate_psum", H * (g - NHT) + H - 1)
            tt(dve, hT["lo"][:, g % NHT, :], bank[:, :], hT["hi"][:, g % NHT, :].bitcast(F32), ALU.subtract,
               ("hT_lo", g))

        def project_q(u, half):
            g, j = divmod(UC * u, GC)
            tokens = slice(j * P, j * P + UW)
            hi, lo = (hT[s][:, g % NHT, tokens] for s in ("hi", "lo"))
            n = 2 * u + half
            bank = take_bank(("swapped", n))
            wait(pe, "w_qk_lo")
            wait(pe, "hT_hi", g)
            wait(pe, "hT_lo", g)
            for k in range(2):
                o = bank[:, k * UW:(k + 1) * UW]
                cols = slice((2 * half + k) * P, (2 * half + k + 1) * P)
                matmul(o, wqk["hi"][:, cols], hi, True, False)
                matmul(o, wqk["hi"][:, cols], lo, False, False)
                matmul(o, wqk["lo"][:, cols], hi, False, True, ("proj_q", n) if k else None)
            psum["q", n] = bank

        def rotate_q(u, half):
            start = (u * UW) % T
            cos, sin = (rotary_q[:, k:k + 1, start:start + UW].broadcast_to([P, 2, UW]) for k in range(2))
            n = 2 * u + half
            bank = psum.pop(("q", n))
            turned, partners = qT[:, u % 2, 2 * half:2 * half + 2, :], swapped[:, n % NSWAP, :, :]
            wait(dve, "const")
            wait(dve, "proj_q", n)
            wait(dve, "qT", n - NSWAP)
            wait(dve, "z_O", UC * (u - 2) + UC - 1)
            wait(dve, "scores_O", UC * (u - 2) + UC - 1)
            tt(dve, turned, by(2, bank[:, :]), cos, ALU.mult, ("cos_q", n))
            emit(dve, lambda e, o=partners, i=by(2, bank[:, :]): e.stream_shuffle(o, i, PARTNERS), ("swapped", n))
            wait(pool, "swapped", n)
            tt(pool, partners, partners, sin, ALU.mult, ("sin_q", n))
            wait(pool, "cos_q", n)
            wait(pool, "sin_q", n)
            tt(pool, turned, turned, partners, ALU.add, ("qT", n))

        def project_k(i):
            g, j = divmod(i, GC)
            hi, lo = (hT[s][:, g % NHT, j * P:(j + 1) * P] for s in ("hi", "lo"))
            cols = slice(H * D, 2 * H * D)
            bank = take_bank(("sin_k", i))
            wait(pe, "w_qk_lo")
            wait(pe, "hT_hi", g)
            wait(pe, "hT_lo", g)
            matmul(bank[:, :], hi, wqk["hi"][:, cols], True, False)
            matmul(bank[:, :], hi, wqk["lo"][:, cols], False, False)
            matmul(bank[:, :], lo, wqk["hi"][:, cols], False, True, ("proj_k", i))
            psum["k", i] = bank

        def rotate_k(i):
            c, bank = i % CB, psum.pop(("k", i))
            turned = rot_k[:, i % 2, :, :]
            wait(dve, "key_tables", c)
            wait(dve, "proj_k", i)
            wait(dve, "state", i - 2)
            wait(dve, "T_k", i - 2)
            tt(dve, turned, by(H, bank[:, :]), kcos[:, c, :, :], ALU.mult, ("cos_k", i))
            wait(dve, "rot_k", i - 1)
            in_quarters = lambda ap: ap.rearrange("p h (k d) -> p (h k) d", k=2).rearrange(
                "p h (k d) -> p h k d", k=2)
            partners = bank[:, :].rearrange("p (h k d) -> p h k d", k=2, d=QUARTER)[:, :, ::-1, :]
            tt(dve, in_quarters(sin_k[:, :, :]), partners, in_quarters(ksin[:, c, :, :]), ALU.mult, ("sin_k", i))
            wait(pool, "cos_k", i)
            wait(pool, "sin_k", i)
            tt(pool, turned, turned, sin_k[:, :, :], ALU.add, ("rot_k", i))

        def transpose_k(i):
            bank = take_bank(("kT", i))
            wait(pe, "rot_k", i)
            flat = rot_k[:, i % 2, :, :].rearrange("p h d -> p (h d)")
            for n in range(PAIRS):
                transpose(bank[:, n * P:(n + 1) * P], flat[:, n * P:(n + 1) * P],
                          ("T_k", i) if n == PAIRS - 1 else None)
            psum["kT", i] = bank

        def copy_kT(i):
            wait(act, "T_k", i)
            wait(act, "scores_O", i - NKT)
            activate(kT[:, i % NKT, :, :], by(PAIRS, psum.pop(("kT", i))[:, :]), ACT.Copy, done=("kT", i))

        def accumulate_state(i):
            g, j = divmod(i, GC)
            if i % CB == CB - 1:
                did["state", i] = did["state", i - 1]
                return
            wait(pe, "S", i - 1 if i % CB else i - 2)
            wait(pe, "rot_k", i)
            wait(pe, "h_nat", g)
            flat = rot_k[:, i % 2, :, :].rearrange("p h d -> p (h d)")
            for n in range(PAIRS):
                matmul(state_bank[:, n * C:(n + 1) * C], flat[:, n * P:(n + 1) * P], h_nat[:, g % NHN, j, :],
                       i % CB == 0 and n == 0, True, ("state", i) if n == PAIRS - 1 else None)

        def copy_state(i):
            if i % CB == CB - 1:
                return
            wait(act, "state", i)
            wait(act, "z_O", i - 1)
            activate(S[:, i % 2, :, :], by(PAIRS, state_bank[:, :]), ACT.Copy, done=("S", i))

        def queries(i, n):
            u, k = divmod(i, UC)
            return qT[:, u % 2, n, k * P:(k + 1) * P]

        def split_h(i):
            g, j = divmod(i, GC)
            h = h_nat[:, g % NHN, j, :]
            hi, lo = (h_split[s][:, i % NSPLIT, :] for s in ("hi", "lo"))
            wait(act, "h_nat", g)
            wait(act, "z_O", i - NSPLIT)
            activate(hi, h, ACT.Copy, ("h_hi", i))
            wait(dve, "h_hi", i)
            wait(dve, "z_O", i - NSPLIT)
            tt(dve, lo, h, hi.bitcast(F32), ALU.subtract, ("h_lo", i))

        def scores(i):
            pair = take_bank(("A_E", i)), take_bank(("A_O", i))
            wait(pe, "qT", 2 * (i // UC) + 1)
            wait(pe, "kT", i)
            for n in range(PAIRS):
                q = queries(i, n)
                for odd, bank in enumerate(pair):
                    rows = slice(odd * D, (odd + 1) * D)
                    matmul(bank[:, n * P:(n + 1) * P], kT[rows, i % NKT, n, :], q[rows, :], True, True,
                           ("scores_" + "EO"[odd], i) if n == PAIRS - 1 else None)
            psum["A", 0, i], psum["A", 1, i] = pair

        def mask_scores(i, odd):
            eo, bank = "EO"[odd], psum.pop(("A", odd, i))
            wait(dve, "scores_" + eo, i)
            wait(dve, "A_hi_" + eo, i - 1)
            wait(dve, "A_lo_" + eo, i - 1)
            tt(dve, A[odd][:, :, :], by(PAIRS, bank[:, :]), causal.unsqueeze(1).broadcast_to([P, PAIRS, P]),
               ALU.mult, ("A_" + eo, i))
            wait(act, "A_" + eo, i)
            wait(act, "z_O", i - NSPLIT)
            activate(by(PAIRS, A_split["hi"][odd][:, i % NSPLIT, :]), A[odd][:, :, :], ACT.Copy, ("A_hi_" + eo, i))

        def split_scores(i, odd):
            eo = "EO"[odd]
            wait(dve, "A_hi_" + eo, i)
            wait(dve, "z_O", i - NSPLIT)
            hi, lo = (by(PAIRS, A_split[s][odd][:, i % NSPLIT, :]) for s in ("hi", "lo"))
            tt(dve, lo, A[odd][:, :, :], hi.bitcast(F32), ALU.subtract, ("A_lo_" + eo, i))

        def mix_tokens(i):
            first = i % CB == 0
            pair = take_bank(("Z_E", i)), take_bank(("Z_O", i))
            h_hi, h_lo = (h_split[s][:, i % NSPLIT, :] for s in ("hi", "lo"))
            wait(pe, "h_lo", i)
            for odd, bank in enumerate(pair):
                A_hi, A_lo = (A_split[s][odd][:, i % NSPLIT, :] for s in ("hi", "lo"))
                wait(pe, "A_lo_" + "EO"[odd], i)
                matmul(bank[:, :], h_hi, A_hi, True, False)
                matmul(bank[:, :], h_hi, A_lo, False, False)
                matmul(bank[:, :], h_lo, A_hi, False, first, ("z_" + "EO"[odd], i) if first else None)
            if not first:
                wait(pe, "S", i - 1)
                for n in range(PAIRS):
                    q = queries(i, n)
                    for odd, bank in enumerate(pair):
                        rows = slice(odd * D, (odd + 1) * D)
                        matmul(bank[:, n * P:(n + 1) * P], S[rows, (i - 1) % 2, n, :], q[rows, :],
                               False, n == PAIRS - 1, ("z_" + "EO"[odd], i) if n == PAIRS - 1 else None)
            psum["Z", i] = pair

        def copy_Z(i):
            for odd, bank in enumerate(psum.pop(("Z", i))):
                wait(act, "z_" + "EO"[odd], i)
                wait(act, "heads_" + "EO"[odd], i - 1)
                activate(Z[odd][:, :, :], by(PAIRS, bank[:, :]), ACT.Copy, done=("Z_" + "EO"[odd], i))

        def head_outputs(i, odd):
            eo = "EO"[odd]
            bank = take_bank(("O_" + eo, i))
            wait(pe, "Z_" + eo, i)
            wait(pe, "w_v")
            for n in range(PAIRS):
                matmul(bank[:, n * V:(n + 1) * V], Z[odd][:, n, :], wv[:, 2 * n + odd, :], True, True,
                       ("heads_" + eo, i) if n == PAIRS - 1 else None)
            psum["O", odd, i] = bank

        def copy_outputs(i, odd):
            wait(act, "heads_" + "EO"[odd], i)
            wait(act, "nT_psum", H * ((i - NN) // GC) + H - 1)
            wait(act, "w_g_lo")
            wait(act, "w_qk_lo")
            activate(N[:, i % NN, odd, :, :], by(PAIRS, psum.pop(("O", odd, i))[:, :]), ACT.Copy, done=("O_" + "EO"[odd], i))

        def head_stats(i, odd):
            s, slot, eo = i % NGN, i % NN, "EO"[odd]
            wait(dve, "gn_apply", i - NGN)
            wait(dve, "O_" + eo, i)
            for n in range(PAIRS):
                k = odd * PAIRS + n
                a, o = N[:, slot, odd, n, :], gn_stats[:, s, k, :]
                emit(dve, lambda e, a=a, o=o: e.bn_stats(o, a), ("gn_stats_" + eo, PAIRS * i + n))
            for n in range(PAIRS):
                k = odd * PAIRS + n
                wait(dve, "gn_stats_" + eo, PAIRS * i + n)
                a, o = gn_stats[:, s, k, :], gn_mv[:, s, k, :]
                emit(dve, lambda e, a=a, o=o: e.bn_aggr(o, a), ("gn_mv_" + eo, i) if n == PAIRS - 1 else None)

        def head_rstd(i):
            s, c = i % NGN, i % CB
            for eo in "EO":
                wait(pool, "gn_mv_" + eo, i)
            wait(pool, "gn_apply", i - NGN)
            eps_eo = norm_eps[:, c, :].rearrange("p (a e) -> p e a", e=2)
            tt(pool, by(2, gn_var[:, s, :]), gn_mv[:, s, :, 1].rearrange("p (e a) -> p e a", e=2), eps_eo, ALU.add,
               ("gn_var", i))
            wait(pool, "gn_var", i)
            tt(pool, gn_rstd[:, s, :], gn_var[:, s, :], minus_half[:, :].broadcast_to([P, H]), ALU.pow,
               ("gn_rstd", i))

        def norm_heads(i):
            s, slot = i % NGN, i % NN
            wait(dve, "gn_rstd", i)
            for k in range(H):
                a = N[:, slot, k // PAIRS, k % PAIRS, :]
                ts(dve, a, a, gn_mv[:, s, k, 0:1], gn_rstd[:, s, k:k + 1], ALU.subtract, ALU.mult,
                   ("gn_apply", i) if k == H - 1 else None)

        def project_gate(n):
            g, h = divmod(n, H)
            cols = slice(h * V, (h + 1) * V)
            hi, lo = (hT[s][:, g % NHT, :] for s in ("hi", "lo"))
            bank = take_bank(("gate", n))
            wait(pe, "w_g_lo")
            matmul(bank[:, :], wg["hi"][:, cols], hi, True, False)
            matmul(bank[:, :], wg["hi"][:, cols], lo, False, False)
            matmul(bank[:, :], wg["lo"][:, cols], hi, False, True, ("gate_psum", n))
            psum["g", n] = bank

        def gate_silu(n):
            wait(act, "gate_psum", n)
            wait(act, "y", n - 2)
            activate(gate[:, n % 2, :], psum.pop(("g", n))[:, :], ACT.Silu, ("gate", n))

        def turn_head(n):
            g, h = divmod(n, H)
            bank = take_bank(("scaled", n))
            wait(pe, "gn_apply", GC * g + GC - 1)
            for j in range(GC):
                transpose(bank[:, j * P:(j + 1) * P], N[:, (GC * g + j) % NN, h % 2, h // 2, :],
                          ("nT_psum", n) if j == GC - 1 else None)
            psum["n", n] = bank

        def scale_head(n):
            h = n % H
            wait(act, "nT_psum", n)
            wait(act, "gn")
            wait(act, "y", n - 2)
            activate(scaled[:, n % 2, :], psum.pop(("n", n))[:, :], ACT.Identity, ("scaled", n),
                     bias=gn[:, 1, h:h + 1], scale=gn[:, 0, h:h + 1])

        def gate_head(n):
            wait(pool, "gate", n)
            wait(pool, "scaled", n)
            wait(pool, "out_head", n - 2)
            tt(pool, y[:, n % 2, :], scaled[:, n % 2, :], gate[:, n % 2, :], ALU.mult, ("y", n))

        def project_out(n):
            g, h = divmod(n, H)
            wait(pe, "w_o")
            wait(pe, "y", n)
            if h == 0:
                wait(pe, "attn", g - 1)
            for j in range(GC):
                matmul(out_bank[:, j * C:(j + 1) * C], y[:, n % 2, j * P:(j + 1) * P], wo[:, h, :],
                       h == 0 and j == 0, h == H - 1, ("out_head", n) if j == GC - 1 else None)

        def residual(g):
            m = mod[:, (g // GB) % NMOD, :, :]
            xg = X[:, g % NX, :, :]
            wait(dve, "out_head", H * g + H - 1)
            wait(dve, "ffn_out", g - 1)
            wait(dve, "mod_gates", g // GB)
            tt(dve, attn[:, :, :], by(GC, out_bank[:, :]), m[:, 2:3, :].broadcast_to([P, GC, C]), ALU.mult,
               ("attn", g))
            wait(pool, "attn", g)
            tt(pool, xg, xg, attn[:, :, :], ALU.add, ("residual", g))

        def transpose_n2(g):
            bank = take_bank(("h2T", g))
            wait(pe, "ln_apply1", g)
            for j in range(GC):
                transpose(bank[:, j * P:(j + 1) * P], normed[:, j, :], ("n2T", g) if j == GC - 1 else None)
            psum["n2", g] = bank

        def modulate2(g):
            b, half = divmod(g, GB)
            bank = psum.pop(("n2", g))
            wait(act, "n2T", g)
            wait(act, "mod_cols")
            wait(act, "mix_k", g - 2)
            wait(act, "h2T_edge", g - 1 if half == 0 else -1)
            activate(h2T[:, half, 1:1 + W], bank[:, :], ACT.Identity, ("h2T", g), bias=mod_cols[:, 0, b:b + 1],
                     scale=mod_cols[:, 1, b:b + 1])
            if half:
                wait(act, "h2T", g - 1)
                activate(h2T[:, half, 0:1], h2T[:, half - 1, W:W + 1], ACT.Copy, ("h2T_edge", g))

        def mix_shift(g):
            half = g % GB
            now, before = h2T[:, half, 1:1 + W], h2T[:, half, 0:W]
            for q in (pool, dve):
                wait(q, "h2T", g)
                if half:
                    wait(q, "h2T_edge", g)
                else:
                    wait(q, "zero_column")
            wait(pool, "mix_k", g - 1)
            wait(pool, "ffn_out", g - 1)
            tt(pool, delta, now, before, ALU.subtract, ("delta", g))
            wait(dve, "delta", g)
            wait(dve, "mu")
            wait(dve, "rk_psum", 2 * (g - 1) + 1)
            for n, what in enumerate("rk"):
                stt(dve, mixed[what][:, :], delta, mu[:, n:n + 1], before, ALU.mult, ALU.add,
                    ("mix_" + what, g))

        def project_r(g):
            bank = take_bank(("r_tanh", g))
            wait(pe, "w_ffn")
            wait(pe, "mix_r", g)
            for j in range(GC):
                matmul(bank[:, j * C:(j + 1) * C], mixed["r"][:, j * P:(j + 1) * P], wffn[:, 0, :], True, True,
                       ("rk_psum", 2 * g) if j == GC - 1 else None)
            psum["r", g] = bank

        def act_r(g):
            wait(act, "rk_psum", 2 * g)
            wait(act, "ffn_product", g - 1)
            activate(r_tanh, by(GC, psum.pop(("r", g))[:, :]), ACT.Tanh, ("r_tanh", g), scale=0.5)

        def project_ffn_k(g):
            bank = take_bank(("relu", g))
            wait(pe, "mix_k", g)
            matmul(bank[:, :], wffn[:, 1, :], mixed["k"][:, :], True, True, ("rk_psum", 2 * g + 1))
            psum["ffn_k", g] = bank

        def act_k(g):
            wait(act, "rk_psum", 2 * g + 1)
            wait(act, "ffn_psum", g - 1)
            activate(k_act[:, :], psum.pop(("ffn_k", g))[:, :], ACT.Relu, ("relu", g))
            wait(act, "relu", g)
            activate(k_act[:, :], k_act[:, :], ACT.Square, ("k_act", g))

        def ffn_gate(g):
            m = mod[:, (g // GB) % NMOD, :, :]
            wait(dve, "r_tanh", g)
            stt(dve, r_tanh, r_tanh, 1.0, m[:, 3:4, :].broadcast_to([P, GC, C]), ALU.add, ALU.mult,
                ("r_gate", g))

        def project_ffn_out(g):
            bank = take_bank(("ffn_product", g))
            wait(pe, "k_act", g)
            for j in range(GC):
                matmul(bank[:, j * C:(j + 1) * C], k_act[:, j * P:(j + 1) * P], wffn[:, 2, :], True, True,
                       ("ffn_psum", g) if j == GC - 1 else None)
            psum["ffn", g] = bank

        def ffn_out(g):
            xg, bank = X[:, g % NX, :, :], psum.pop(("ffn", g))
            wait(dve, "ffn_psum", g)
            wait(dve, "r_gate", g)
            wait(dve, "residual", g)
            wait(dve, "ffn_out", g - 1)
            stt(dve, attn[:, :, :], by(GC, bank[:, :]), 0.5, r_tanh, ALU.mult, ALU.mult, ("ffn_product", g))
            wait(pool, "ffn_product", g)
            tt(pool, xg, xg, attn[:, :, :], ALU.add, ("ffn_out", g))
            wait(sp, "ffn_out", g)
            dma(sp, out_rows[g], xg, ("out%d" % (g % NX), g // NX))

        def one(f):
            return 1, NCHUNK, f

        def group(f):
            return GC, NGROUP, f

        def head(f):
            return 1, NCHUNK, f

        stages = {
            "key_tables": (1, CB, key_tables),
            "project_k": one(project_k), "rotate_k": one(rotate_k),
            "transpose_k": one(transpose_k), "copy_kT": one(copy_kT),
            "state": one(accumulate_state), "copy_state": one(copy_state),
            "split_h": one(split_h), "scores": one(scores),
            "mix": one(mix_tokens), "copy_Z": one(copy_Z), "head_rstd": one(head_rstd),
            "norm_heads": one(norm_heads),
            "transpose_h": group(transpose_h), "split_hT": group(split_hT),
            "norm_stats0": group(lambda g: norm_stats(g, 0)), "norm_apply0": group(lambda g: norm_apply(g, 0)),
            "modulate": group(modulate),
            "mod_input": (GB * GC, B, mod_input), "mod_rows": (GB * GC, B, mod_rows),
            "residual": group(residual), "norm_stats1": group(lambda g: norm_stats(g, 1)),
            "norm_apply1": group(lambda g: norm_apply(g, 1)), "transpose_n2": group(transpose_n2),
            "modulate2": group(modulate2), "mix_shift": group(mix_shift), "project_r": group(project_r),
            "act_r": group(act_r), "project_ffn_k": group(project_ffn_k), "act_k": group(act_k),
            "ffn_gate": group(ffn_gate), "project_ffn_out": group(project_ffn_out), "ffn_out": group(ffn_out),
            "load_x": (GC, NGROUP - NX, lambda g: load_x(g + NX)),
        }
        for n in range(2):
            for name, f in (("project_q", project_q), ("rotate_q", rotate_q)):
                stages[f"{name}_{n}"] = (UC, NCHUNK // UC, lambda u, f=f, n=n: f(u, n))
            for name, f in (("mask", mask_scores), ("split", split_scores), ("head_outputs", head_outputs),
                            ("copy_outputs", copy_outputs), ("head_stats", head_stats)):
                stages[f"{name}_{'EO'[n]}"] = one(lambda i, f=f, n=n: f(i, n))
            for name, f in (("project_gate", project_gate), ("gate_silu", gate_silu), ("turn_head", turn_head),
                            ("scale_head", scale_head), ("gate_head", gate_head), ("project_out", project_out)):
                stages[f"{name}_{n}"] = (1, NCHUNK, lambda i, f=f, n=n: f(2 * i + n))

        queued = set()

        def queue(name, n):
            if (name, n) not in queued:
                queued.add((name, n))
                stages[name][2](n)

        prologue_loads()
        prologue()
        for name in PROLOGUE:
            if name in stages:
                queue(name, 0)
            elif name == "mod_columns":
                mod_columns()
            elif name == "split_w_qk":
                split_weights("w_qk", raw_qk, wqk)
            elif name == "split_w_g":
                split_weights("w_g", raw_g, wg)
        last = max(lag + stages[name][0] * (stages[name][1] - 1) for name, lag in ORDER)
        for step in range(min(lag for name, lag in ORDER), last + 1):
            for name, lag in ORDER:
                every, many, _ = stages[name]
                n, rest = divmod(step - lag, every)
                if rest == 0 and 0 <= n < many:
                    queue(name, n)
        for g in range(max(0, NGROUP - NX), NGROUP):
            wait_stored(g)

        block = ctx.enter_context(nc.Block())

        @block.tensor
        def _(e):
            for f in pe:
                f(e)

        @block.scalar
        def _(e):
            for f in act:
                f(e)

        @block.vector
        def _(e):
            for f in dve:
                f(e)

        @block.gpsimd
        def _(e):
            for f in pool:
                f(e)

        @block.sync
        def _(e):
            for f in sp:
                f(e)


def kernel(L0_attn_x, L0_attn_Wq, L0_attn_Wk, L0_attn_Wv, L0_attn_Wg, L0_attn_Wo, L0_attn_gn_weight,
           L0_attn_gn_bias, L0_ffn_W_r, L0_ffn_W_k, L0_ffn_W_v, L0_ffn_mu_r, L0_ffn_mu_k, L0_c, L0_wmod):
    import concourse.bacc as bacc
    from concourse.bass_utils import run_bass_kernel_spmd

    def a(v):
        return np.asarray(v)

    def quarters(w):
        return w.reshape(H, 2, 2, QUARTER, C).transpose(0, 2, 1, 3, 4).reshape(H * D, C)

    lay = np.ascontiguousarray
    arrays = {
        "x": lay(a(L0_attn_x)),
        "cT": lay(a(L0_c).T),
        "w_mod": lay(a(L0_wmod)),
        "w_qkT": lay(np.concatenate([quarters(a(L0_attn_Wq)), quarters(a(L0_attn_Wk))], 0).T),
        "w_gT": lay(a(L0_attn_Wg).T),
        "w_vT": lay(a(L0_attn_Wv).T),
        "w_oT": lay(a(L0_attn_Wo).T.reshape(H, V, C).transpose(1, 0, 2).reshape(V, H * C)),
        "norm_wb": lay(np.stack([a(L0_attn_gn_weight), a(L0_attn_gn_bias)]).reshape(2, H, V).transpose(2, 0, 1)),
        "w_ffnT": lay(np.concatenate([a(L0_ffn_W_r).T, a(L0_ffn_W_k).T, a(L0_ffn_W_v).T], 1)),
        "ffn_mu": lay(np.stack([a(L0_ffn_mu_r), a(L0_ffn_mu_k)], 1)),
        "const": constants(),
    }
    nc = bacc.Bacc("TRN2", target_bir_lowering=False, num_devices=1)
    ins = [nc.dram_tensor("in_" + n, v.shape, mybir.dt.from_np(v.dtype), kind="ExternalInput").ap()
           for n, v in arrays.items()]
    out = nc.dram_tensor("out", (B, T, C), F32, kind="ExternalOutput").ap()
    build(nc, *ins, out)
    r = run_bass_kernel_spmd(nc, [{"in_" + n: v for n, v in arrays.items()}], core_ids=[0])
    return r.results[0]["out"]
```

```python
from contextlib import ExitStack

import numpy as np

import concourse.bass as bass
from concourse import mybir

F32 = mybir.dt.float32
F32R = mybir.dt.float32r
ALU = mybir.AluOpType
ACT = mybir.ActivationFunctionType

P = 128
B, T, C = 8, 1024, 128
H, D, V = 8, 64, 128
PAIRS = H // 2
QUARTER = D // 4
GC = 4
NCHUNK = B * T // P
NGROUP = NCHUNK // GC
CB = T // P
GB = CB // GC
W = GC * P
EPS = 1e-5
MID = T // 2
UC = 2
UW = UC * P

NX, NHT, NHN, NMOD, NN = 5, 3, 2, 3, 2 * GC
NKT, NSPLIT, NGN, NSWAP, NY = 1, 1, 2, 2, 3
FAST_UNITS = 1

HEAD_END, TAIL_START = 6, NCHUNK - 1
PROLOGUE = ["mod_input", "mod_rows", "mod_columns", "norm_stats0", "split_w_qk", "norm_apply0", "modulate",
    "split_w_g", "key_tables", "transpose_h", "split_hT", "project_q_0", "split_w_o", "project_k",
    "project_q_1", "rotate_k", "rotate_q_0", "rotate_q_1"]
HEAD_ORDER = [("split_y_lo_1", 7), ("mix", 1), ("copy_Z", 1), ("norm_stats0", -4), ("project_k", -1),
    ("mix_shift", 11), ("rotate_q_0", -1), ("turn_head_0", 5), ("transpose_h", -2), ("ffn_gate", 11),
    ("project_q_1", -1), ("norm_apply1", 13), ("rotate_k", -1), ("split_h", 0), ("scale_head_0", 5),
    ("act_r", 13), ("mod_input", -7), ("split_hT", -2), ("split_y_hi_1", 8), ("norm_heads_O", 2),
    ("head_outputs_O", 1), ("copy_outputs_O", 1), ("ffn_out", 12), ("turn_head_1", 5), ("gate_head_0", 5),
    ("rotate_q_1", -1), ("scale_head_1", 5), ("head_stats_O", 1), ("project_out_1", 6), ("head_outputs_E", 1),
    ("modulate2", 9), ("copy_outputs_E", 1), ("split_y_hi_0", 5), ("scores", 0), ("project_ffn_k", 13),
    ("head_stats_E", 1), ("copy_state", 0), ("head_rstd", 1), ("load_x", 17), ("transpose_n2", 11),
    ("project_q_0", -2), ("split_y_lo_0", 5), ("mask_E", 0), ("transpose_k", -1), ("project_gate_1", 5),
    ("state", -1), ("norm_apply0", -4), ("residual", 10), ("act_k", 13), ("mask_O", 0), ("split_E", 0),
    ("gate_silu_1", 5), ("project_gate_0", 4), ("gate_silu_0", 4), ("split_O", 0), ("gate_head_1", 5),
    ("project_ffn_out", 12), ("mod_rows", -5), ("project_r", 13), ("project_out_0", 5), ("norm_heads_E", 1),
    ("turn_attn", 7), ("norm_stats1", 8), ("key_tables", -2), ("copy_kT", -1), ("modulate", -4),
    ("scale_attn", 13)]
ORDER = [("turn_head_0", 5), ("modulate", -3), ("norm_heads_O", 2), ("rotate_q_0", -1), ("norm_stats1", 10),
    ("mod_rows", -4), ("ffn_gate", 13), ("split_y_hi_1", 6), ("ffn_out", 13), ("norm_apply1", 11),
    ("scale_head_0", 5), ("split_y_lo_1", 6), ("mix", 1), ("project_k", -1), ("gate_head_0", 5), ("copy_Z", 1),
    ("project_q_1", -1), ("transpose_h", -2), ("rotate_k", -1), ("split_hT", -2), ("project_out_1", 6),
    ("split_h", 0), ("norm_stats0", -4), ("head_outputs_O", 1), ("copy_state", 0), ("rotate_q_1", -1),
    ("key_tables", -2), ("copy_outputs_O", 1), ("scale_attn", 9), ("head_outputs_E", 1), ("transpose_n2", 11),
    ("copy_outputs_E", 1), ("mod_input", -6), ("turn_head_1", 5), ("head_stats_O", 1), ("scores", 0),
    ("project_gate_1", 5), ("scale_head_1", 5), ("turn_attn", 9), ("modulate2", 11), ("split_y_hi_0", 5),
    ("head_stats_E", 1), ("project_r", 12), ("project_gate_0", 4), ("transpose_k", -1), ("mask_E", 0),
    ("mask_O", 0), ("head_rstd", 1), ("project_ffn_k", 12), ("gate_silu_1", 5), ("state", -1),
    ("gate_silu_0", 4), ("act_k", 12), ("split_y_lo_0", 5), ("residual", 9), ("project_q_0", -2),
    ("project_out_0", 5), ("norm_apply0", -4), ("split_E", 0), ("split_O", 0), ("load_x", 13),
    ("norm_heads_E", 1), ("act_r", 12), ("mix_shift", 11), ("gate_head_1", 5), ("project_ffn_out", 12),
    ("copy_kT", -1)]
TAIL_ORDER = [("ffn_gate", 13), ("norm_heads_E", 2), ("gate_head_1", 6), ("mix_shift", 12), ("norm_apply0", -3),
    ("project_out_0", 6), ("residual", 10), ("norm_apply1", 11), ("project_ffn_out", 13), ("ffn_out", 13),
    ("mix", 1), ("norm_heads_O", 2), ("split_y_hi_1", 6), ("project_q_1", 0), ("turn_head_0", 5),
    ("project_k", -1), ("project_r", 12), ("copy_Z", 1), ("transpose_k", -5), ("transpose_n2", 11),
    ("rotate_k", 1), ("project_q_0", -1), ("split_y_lo_1", 6), ("head_outputs_O", 1), ("head_outputs_E", 1),
    ("scale_head_0", 5), ("act_r", 12), ("mod_rows", -9), ("project_out_1", 6), ("split_h", -2),
    ("rotate_q_1", 2), ("copy_outputs_O", 1), ("scores", 0), ("turn_head_1", 5), ("gate_head_0", 5),
    ("copy_kT", 1), ("head_stats_O", 1), ("modulate2", 11), ("state", -6), ("project_gate_1", 5),
    ("copy_outputs_E", 1), ("modulate", 2), ("head_stats_E", 1), ("transpose_h", -1), ("split_y_hi_0", 5),
    ("scale_attn", 9), ("mask_O", 0), ("copy_state", -3), ("norm_stats0", -5), ("turn_attn", 9),
    ("head_rstd", 1), ("rotate_q_0", -2), ("mask_E", 0), ("split_O", 0), ("project_gate_0", 4),
    ("scale_head_1", 5), ("norm_stats1", 10), ("split_y_lo_0", 5), ("split_E", 0), ("split_hT", -6),
    ("gate_silu_1", 5), ("project_ffn_k", 12), ("gate_silu_0", 4), ("load_x", 15), ("act_k", 12),
    ("key_tables", 1), ("mod_input", -7)]


PARTNERS = [(n + QUARTER) % (2 * QUARTER) for n in range(2 * QUARTER)]


def constants():
    inv_freq = (np.float32(1.0) / np.float32(10000.0) ** (np.arange(0, D, 2, dtype=np.float32) / np.float32(D)))
    angle = (np.arange(T, dtype=np.float32)[:, None] * inv_freq.astype(np.float32)[None, :]).astype(np.float32)
    cos, sin = np.cos(angle), np.sin(angle)
    tables = np.stack([np.concatenate([cos, cos], 1), np.concatenate([-sin, sin], 1)])
    tables = tables.reshape(2, T, 2, 2, QUARTER).transpose(0, 1, 3, 2, 4).reshape(2, T, D)
    cosines = tables[0].reshape(T, 2, 2, QUARTER)[:, :, 0, :]
    rotary_q = np.concatenate([tables, tables], 2).transpose(2, 0, 1).reshape(P, 2 * T)
    gamma = 1.0 - np.exp2(-5.0 - np.arange(H, dtype=np.float64))
    away = MID - np.arange(T, dtype=np.float64)
    key_decay = gamma[None, :] ** away[:, None]
    norm_eps = EPS * D * key_decay ** 2
    causal = (np.arange(P)[:, None] <= np.arange(P)[None, :])
    by_partition = lambda a: a.reshape(CB, P, -1).transpose(1, 0, 2).reshape(P, -1)
    parts = [by_partition(cosines), by_partition(tables[1]), by_partition(key_decay), by_partition(norm_eps), causal, np.eye(P)]
    return np.concatenate(parts, 1).astype(np.float32), rotary_q.astype(np.float32)


def build(nc, x, cT, w_mod, w_qkT, w_gT, w_vT, w_oT, norm_wb, w_ffnT, ffn_mu, const, const_q, out):
    with ExitStack() as ctx:
        def sb(name, shape, dt=F32):
            return ctx.enter_context(nc.sbuf_tensor(name, shape, dt))

        def by(n, ap):
            return ap.rearrange("p (a b) -> p a b", a=n)

        n_const = const.shape[1]
        consts = sb("consts", [P, n_const])
        at = [0]

        def const_part(n):
            at[0] += n
            return consts[:, at[0] - n:at[0]]

        cosines = const_part(CB * D // 2).rearrange("p (c d) -> p c d", c=CB)
        sines = const_part(CB * D).rearrange("p (c d) -> p c d", c=CB)
        key_decay = const_part(CB * H).rearrange("p (c h) -> p c h", c=CB)
        norm_eps = const_part(CB * H).rearrange("p (c h) -> p c h", c=CB)
        causal = const_part(P)
        ident = const_part(P)
        rotary_q = sb("rotary_q", [P, 2, T])

        X = sb("X", [P, NX, GC, C])
        kcos = sb("kcos", [P, CB, H, D // 2])
        ksin = sb("ksin", [P, CB, H, D])
        wqk = {s: sb("wqk_" + s, [P, 2 * H * D], F32R) for s in ("hi", "lo")}
        wg = {s: sb("wg_" + s, [P, H * V], F32R) for s in ("hi", "lo")}
        wv = sb("wv", [P, H, V])
        wo = {s: sb("wo_" + s, [P, H * C], F32R) for s in ("hi", "lo")}
        wffn = sb("wffn", [P, 3, C])
        mu = sb("mu", [P, 2])
        gn = sb("gn", [P, 2, H])
        wmod = sb("wmod", [P, 6 * C])
        cond = sb("cond", [P, B])
        silu_c = sb("silu_c", [P, B])
        silu_rows = sb("silu_rows", [P, P])
        mod = sb("mod", [P, NMOD, 3, C])
        mod_pos = sb("mod_pos", [P, C])
        mod_neg = sb("mod_neg", [P, C])
        mod_cols = sb("mod_cols", [P, 3, B])
        minus_half = sb("minus_half", [P, 1])
        eps = sb("eps", [P, 1])
        warm = sb("warm", [P, 1])

        ln_stats = sb("ln_stats", [P, 2, GC, 6])
        ln_mv = sb("ln_mv", [P, 2, GC, 2])
        ln_var = sb("ln_var", [P, 2, GC])
        ln_rstd = sb("ln_rstd", [P, 2, GC])
        normed = sb("normed", [P, GC, C])
        h_nat = sb("h_nat", [P, NHN, GC, C])
        hT = {s: sb("hT_" + s, [P, NHT, W], F32R) for s in ("hi", "lo")}

        rot_k = sb("rot_k", [P, 2, H, D])
        sin_k = sb("sin_k", [P, H, D])
        kT = sb("kT", [P, NKT, PAIRS, P])
        swapped = sb("swapped", [P, NSWAP, 2, UW])
        qT = sb("qT", [P, 2, PAIRS, UW])
        S = sb("S", [P, 2, PAIRS, C])
        h_split = {s: sb("h_" + s, [P, NSPLIT, C], F32R) for s in ("hi", "lo")}
        A = [sb(f"A{e}", [P, PAIRS, P]) for e in range(2)]
        A_split = {s: [sb(f"A{e}_{s}", [P, NSPLIT, W], F32R) for e in range(2)] for s in ("hi", "lo")}
        Z = [sb(f"Z{e}", [P, PAIRS, P]) for e in range(2)]
        N = sb("N", [P, NN, 2, PAIRS, V])
        gn_stats = sb("gn_stats", [P, NGN, H, 6])
        gn_mv = sb("gn_mv", [P, NGN, H, 2])
        gn_var = sb("gn_var", [P, NGN, H])
        gn_rstd = sb("gn_rstd", [P, NGN, H])
        gn_shift = sb("gn_shift", [P, PAIRS])
        gate = sb("gate", [P, 2, W])
        scaled = sb("scaled", [P, NY, W])
        y_split = {s: sb("y_" + s, [P, 2, W], F32R) for s in ("hi", "lo")}

        attn = sb("attn", [P, GC, C])
        h2T = sb("h2T", [P, GB, 1 + W])
        delta = attn_flat = attn[:, :, :].rearrange("p a b -> p (a b)")
        mixed = {"r": sb("mix_r", [P, W]), "k": sb("mix_k", [P, W])}
        k_act = sb("k_act", [P, W])
        r_tanh = by(GC, mixed["r"][:, :])

        banks = [ctx.enter_context(nc.psum_tensor(f"bank{n}", [P, W], F32)) for n in range(8)]
        state_bank, out_bank = banks[6], banks[7]
        ring = list(range(6))

        pe, act, dve, pool, sp = [], [], [], [], []
        semaphores, count, did, waited, latest = {}, {}, {}, {}, {}

        def promise(done, step=1):
            name, index = done
            if name not in semaphores:
                semaphores[name] = ctx.enter_context(nc.semaphore(name))
                count[name] = 0
            count[name] += step
            assert index > latest.get(name, -1)
            latest[name] = index
            did[done] = (name, count[name])

        def emit(queue, make, done=None, step=1):
            if done is None:
                queue.append(lambda e: make(e))
            else:
                promise(done, step)
                s = semaphores[done[0]]
                queue.append(lambda e: make(e).then_inc(s, step))

        def wait(queue, name, index=0):
            if index < 0:
                return
            sem, value = did[name, index]
            if waited.get((id(queue), sem), 0) >= value:
                return
            waited[id(queue), sem] = value
            s = semaphores[sem]
            queue.append(lambda e: e.wait_ge(s, value))

        def matmul(o, lhsT, rhs, start, stop, done=None):
            emit(pe, lambda e: e.matmul(o, lhsT, rhs, start=start, stop=stop, skip_group_check=True), done)

        def transpose(o, i, done=None):
            emit(pe, lambda e: e.transpose(o, i, ident), done)

        def activate(o, i, func, done=None, **kw):
            emit(act, lambda e: e.activation(o, i, func, **kw), done)

        def tt(q, o, a, b, op, done=None):
            emit(q, lambda e: e.tensor_tensor(o, a, b, op), done)

        def ts(q, o, a, s1, s2, op0, op1=None, done=None):
            if op1 is None:
                emit(q, lambda e: e.tensor_scalar(o, a, s1, s2, op0), done)
            else:
                emit(q, lambda e: e.tensor_scalar(o, a, s1, s2, op0, op1), done)

        def stt(q, o, a, s, b, op0, op1, done=None):
            emit(q, lambda e: e.scalar_tensor_tensor(out=o, in0=a, scalar=s, in1=b, op0=op0, op1=op1), done)

        def dma(q, o, i, done):
            emit(q, lambda e: e.dma_start(o, i), done, 16)

        psum = {}
        last_reader = {}

        def take_bank(freed_by):
            n = ring.pop(0)
            ring.append(n)
            if n in last_reader:
                wait(pe, *last_reader[n])
            last_reader[n] = freed_by
            return banks[n]

        x_rows = x.rearrange("b (g j p) c -> (b g) p j c", j=GC, p=P)
        out_rows = out.rearrange("b (g j p) c -> (b g) p j c", j=GC, p=P)

        def wait_stored(g):
            wait(sp, "out%d" % (g % NX), g // NX)

        def load_x(g):
            wait_stored(g - NX)
            dma(sp, X[:, g % NX, :, :], x_rows[g], ("x%d" % (g % NX), g // NX))

        def wait_x(q, g):
            wait(q, "x%d" % (g % NX), g // NX)

        raw = N[:, :, :, :, :].rearrange("p n e a v -> p (n e a v)")
        raw_qk, raw_g, raw_o = (raw[:, n * 2 * H * D:(n + 1) * 2 * H * D] for n in range(3))

        def prologue_loads():
            load_x(0)
            dma(sp, raw_qk, w_qkT, ("w_qk", 0))
            dma(sp, rotary_q[:, :, :].rearrange("p k t -> p (k t)"), const_q, ("const_q", 0))
            dma(sp, raw_g, w_gT, ("w_g", 0))
            dma(act, cond[:, :], cT, ("cond", 0))
            dma(act, wmod[:, :], w_mod, ("w_mod", 0))
            dma(act, consts[:, :], const, ("const", 0))
            dma(act, wv[:, :, :].rearrange("p h v -> p (h v)"), w_vT, ("w_v", 0))
            dma(sp, gn[:, :, :], norm_wb, ("gn", 0))
            dma(sp, raw_o, w_oT, ("w_o", 0))
            dma(sp, wffn[:, :, :].rearrange("p h v -> p (h v)"), w_ffnT, ("w_ffn", 0))
            dma(sp, mu[:, :], ffn_mu, ("mu", 0))
            for g in range(1, NX):
                load_x(g)

        def prologue():
            emit(pool, lambda e: e.memset(minus_half[:, :], -0.5))
            emit(pool, lambda e: e.memset(eps[:, :], EPS), ("small_consts", 0))
            emit(pool, lambda e: e.memset(h2T[:, 0, 0:1], 0.0), ("zero_column", 0))
            wait(pool, "small_consts")
            wait(act, "small_consts")
            activate(warm[:, :], eps[:, :], ACT.Silu)
            wait(act, "cond")
            activate(silu_c[:, :], cond[:, :], ACT.Silu, ("silu_c", 0))

        def split_weights(name, raw_w, parts):
            wait(act, name)
            activate(parts["hi"][:, :], raw_w, ACT.Copy, (name + "_hi", 0))
            wait(dve, name + "_hi")
            tt(dve, parts["lo"][:, :], raw_w, parts["hi"][:, :].bitcast(F32), ALU.subtract, (name + "_lo", 0))

        def from_zero(o, raw, n, name, index, done):
            pos, neg = mod_pos[:, :n], mod_neg[:, :n]
            ts(dve, pos, raw, 0.25, None, ALU.max, done=(name + "_pos", index))
            ts(dve, neg, raw, -0.25, None, ALU.min, done=(name + "_neg", index))
            wait(dve, name + "_pos", index)
            stt(dve, pos, raw, 0.0, pos, ALU.is_ge, ALU.mult)
            wait(dve, name + "_neg", index)
            stt(dve, neg, raw, 0.0, neg, ALU.is_lt, ALU.mult, (name + "_read", index))
            wait(dve, name + "_read", index)
            tt(dve, o, pos, neg, ALU.add, done)

        def mod_columns():
            bank = take_bank(("mod_cols_read", 0))
            wait(pe, "silu_c")
            wait(pe, "w_mod")
            for n, k in enumerate((3, 4, 2)):
                matmul(bank[:, n * B:(n + 1) * B], wmod[:, k * C:(k + 1) * C], silu_c[:, :], True, True,
                       ("mod_cols_psum", n))
            wait(dve, "mod_cols_psum", 2)
            wait(dve, "mod_gates", 0)
            ts(dve, mod_cols[:, 0, :], bank[:, 0:B], 0.0, None, ALU.add)
            ts(dve, mod_cols[:, 1, :], bank[:, B:2 * B], 1.0, None, ALU.add)
            from_zero(mod_cols[:, 2, :], bank[:, 2 * B:3 * B], B, "mod_cols", 0, ("mod_cols", 0))

        def mod_input(b):
            wait(dve, "silu_c")
            wait(dve, "mod_psum", b - 1)
            ts(dve, silu_rows[:, :], silu_c[:, b:b + 1].broadcast_to([P, P]), 0.0, None, ALU.add,
               done=("silu_rows", b))

        def mod_rows(b):
            m = mod[:, b % NMOD, :, :]
            bank = take_bank(("mod_rows_read", b))
            wait(pe, "w_mod")
            wait(pe, "silu_rows", b)
            matmul(bank[:, 0:2 * C], silu_rows[:, :], wmod[:, 0:2 * C], True, True)
            matmul(bank[:, 2 * C:3 * C], silu_rows[:, :], wmod[:, 5 * C:6 * C], True, True, ("mod_psum", b))
            wait(dve, "mod_psum", b)
            wait(dve, "ffn_out", GB * (b - NMOD) + GB - 1)
            wait(dve, "mod_gates", b - 1)
            if b:
                wait(dve, "mod_cols")
            ts(dve, m[:, 0, :], bank[:, 0:C], 0.0, None, ALU.add)
            ts(dve, m[:, 1, :], bank[:, C:2 * C], 1.0, None, ALU.add, done=("mod_shift", b))
            from_zero(m[:, 2, :], bank[:, 2 * C:3 * C], C, "mod_rows", b, ("mod_gates", b))

        def key_tables(c):
            wait(pool, "const")
            for table, angles, n in ((kcos, cosines, D // 2), (ksin, sines, D)):
                tt(pool, table[:, c, :, :], angles[:, c, :].unsqueeze(1).broadcast_to([P, H, n]),
                   key_decay[:, c, :].unsqueeze(2).broadcast_to([P, H, n]), ALU.mult,
                   ("key_tables", c) if n == D else None)

        def norm_stats(g, which):
            if which == 0:
                wait_x(dve, g)
            else:
                wait(dve, "residual", g)
            wait(dve, f"ln_apply{which}", g - 1)
            for j in range(GC):
                i, o = X[:, g % NX, j, :], ln_stats[:, which, j, :]
                emit(dve, lambda e, i=i, o=o: e.bn_stats(o, i), (f"ln_stats{which}", GC * g + j))
            for j in range(GC):
                wait(dve, f"ln_stats{which}", GC * g + j)
                i, o = ln_stats[:, which, j, :], ln_mv[:, which, j, :]
                emit(dve, lambda e, i=i, o=o: e.bn_aggr(o, i), (f"ln_mv{which}", GC * g + j))
            wait(pool, f"ln_mv{which}", GC * g + GC - 1)
            tt(pool, ln_var[:, which, :], ln_mv[:, which, :, 1], eps[:, :].broadcast_to([P, GC]), ALU.add,
               (f"ln_var{which}", g))
            wait(pool, f"ln_var{which}", g)
            tt(pool, ln_rstd[:, which, :], ln_var[:, which, :], minus_half[:, :].broadcast_to([P, GC]), ALU.pow,
               (f"ln_rstd{which}", g))

        normed_users = []

        def norm_apply(g, which):
            wait(dve, f"ln_rstd{which}", g)
            if normed_users:
                wait(dve, *normed_users[-1])
            normed_users.append((("h_scaled", "n2T")[which], g))
            for j in range(GC):
                ts(dve, normed[:, j, :], X[:, g % NX, j, :], ln_mv[:, which, j, 0:1], ln_rstd[:, which, j:j + 1],
                   ALU.subtract, ALU.mult, (f"ln_apply{which}", g) if j == GC - 1 else None)

        def modulate(g):
            m, h = mod[:, (g // GB) % NMOD, :, :], h_nat[:, g % NHN, :, :]
            q = pool if g else dve
            wait(q, "ln_apply0", g)
            wait(q, "mod_shift", g // GB)
            for used in ("z_O", "state", "hT_psum"):
                wait(q, used, GC * (g - NHN) + GC - 1)
            tt(q, h, normed[:, :, :], m[:, 1:2, :].broadcast_to([P, GC, C]), ALU.mult, ("h_scaled", g))
            wait(q, "h_scaled", g)
            tt(q, h, h, m[:, 0:1, :].broadcast_to([P, GC, C]), ALU.add, ("h_nat", g))

        def transpose_h(g):
            bank = take_bank(("hT_lo", g))
            wait(pe, "h_nat", g)
            wait(pe, "const")
            for j in range(GC):
                transpose(bank[:, j * P:(j + 1) * P], h_nat[:, g % NHN, j, :], ("hT_psum", GC * g + j))
            psum["hT", g] = bank

        def split_hT(g):
            bank = psum.pop(("hT", g))
            wait(act, "hT_psum", GC * g + GC - 1)
            wait(act, "gate_psum", H * (g - NHT) + H - 1)
            activate(hT["hi"][:, g % NHT, :], bank[:, :], ACT.Copy, ("hT_hi", g))
            wait(dve, "hT_hi", g)
            wait(dve, "gate_psum", H * (g - NHT) + H - 1)
            tt(dve, hT["lo"][:, g % NHT, :], bank[:, :], hT["hi"][:, g % NHT, :].bitcast(F32), ALU.subtract,
               ("hT_lo", g))

        def project_q(u, half):
            g, j = divmod(UC * u, GC)
            tokens = slice(j * P, j * P + UW)
            hi, lo = (hT[s][:, g % NHT, tokens] for s in ("hi", "lo"))
            n = 2 * u + half
            bank = take_bank(("swapped", n))
            wait(pe, "w_qk_lo")
            wait(pe, "hT_hi", g)
            wait(pe, "hT_lo", g)
            for k in range(2):
                o = bank[:, k * UW:(k + 1) * UW]
                cols = slice((2 * half + k) * P, (2 * half + k + 1) * P)
                matmul(o, wqk["hi"][:, cols], hi, True, False)
                matmul(o, wqk["hi"][:, cols], lo, False, False)
                matmul(o, wqk["lo"][:, cols], hi, False, True, ("proj_q", n) if k else None)
            psum["q", n] = bank

        def rotate_q(u, half):
            start = (u * UW) % T
            cos, sin = (rotary_q[:, k:k + 1, start:start + UW].broadcast_to([P, 2, UW]) for k in range(2))
            n = 2 * u + half
            bank = psum.pop(("q", n))
            turned, partners = qT[:, u % 2, 2 * half:2 * half + 2, :], swapped[:, n % NSWAP, :, :]
            wait(dve, "const_q")
            wait(dve, "proj_q", n)
            wait(dve, "qT", n - NSWAP)
            wait(dve, "z_O", UC * (u - 2) + UC - 1)
            wait(dve, "scores_O", UC * (u - 2) + UC - 1)
            tt(dve, turned, by(2, bank[:, :]), cos, ALU.mult, ("cos_q", n))
            emit(dve, lambda e, o=partners, i=by(2, bank[:, :]): e.stream_shuffle(o, i, PARTNERS), ("swapped", n))
            q = dve if u < FAST_UNITS else pool
            wait(q, "swapped", n)
            tt(q, partners, partners, sin, ALU.mult, ("sin_q", n))
            wait(q, "cos_q", n)
            wait(q, "sin_q", n)
            tt(q, turned, turned, partners, ALU.add, ("qT", n))

        def project_k(i):
            g, j = divmod(i, GC)
            hi, lo = (hT[s][:, g % NHT, j * P:(j + 1) * P] for s in ("hi", "lo"))
            cols = slice(H * D, 2 * H * D)
            bank = take_bank(("sin_k", i))
            wait(pe, "w_qk_lo")
            wait(pe, "hT_hi", g)
            wait(pe, "hT_lo", g)
            matmul(bank[:, :], hi, wqk["hi"][:, cols], True, False)
            matmul(bank[:, :], hi, wqk["lo"][:, cols], False, False)
            matmul(bank[:, :], lo, wqk["hi"][:, cols], False, True, ("proj_k", i))
            psum["k", i] = bank

        def rotate_k(i):
            c, bank = i % CB, psum.pop(("k", i))
            turned = rot_k[:, i % 2, :, :]
            wait(dve, "key_tables", c)
            wait(dve, "proj_k", i)
            wait(dve, "state", i - 2)
            wait(dve, "T_k", i - 2)
            in_quarters = lambda ap: ap.rearrange("p h (k d) -> p (h k) d", k=2).rearrange(
                "p h (k d) -> p h k d", k=2)
            k = bank[:, :].rearrange("p (h k d) -> p h k d", k=2, d=QUARTER)
            cos = kcos[:, c, :, :].rearrange("p h (k d) -> p (h k) d", k=2).unsqueeze(2)
            tt(dve, in_quarters(turned), k, cos.broadcast_to([P, 2 * H, 2, QUARTER]), ALU.mult, ("cos_k", i))
            wait(dve, "rot_k", i - 1)
            tt(dve, in_quarters(sin_k[:, :, :]), k[:, :, ::-1, :], in_quarters(ksin[:, c, :, :]), ALU.mult,
               ("sin_k", i))
            wait(pool, "cos_k", i)
            wait(pool, "sin_k", i)
            tt(pool, turned, turned, sin_k[:, :, :], ALU.add, ("rot_k", i))

        def transpose_k(i):
            bank = take_bank(("kT", i))
            wait(pe, "rot_k", i)
            flat = rot_k[:, i % 2, :, :].rearrange("p h d -> p (h d)")
            for n in range(PAIRS):
                transpose(bank[:, n * P:(n + 1) * P], flat[:, n * P:(n + 1) * P],
                          ("T_k", i) if n == PAIRS - 1 else None)
            psum["kT", i] = bank

        def copy_kT(i):
            wait(act, "T_k", i)
            wait(act, "scores_O", i - NKT)
            activate(kT[:, i % NKT, :, :], by(PAIRS, psum.pop(("kT", i))[:, :]), ACT.Copy, done=("kT", i))

        def accumulate_state(i):
            g, j = divmod(i, GC)
            if i % CB == CB - 1:
                did["state", i] = did["state", i - 1]
                return
            wait(pe, "S", i - 1 if i % CB else i - 2)
            wait(pe, "rot_k", i)
            wait(pe, "h_nat", g)
            flat = rot_k[:, i % 2, :, :].rearrange("p h d -> p (h d)")
            for n in range(PAIRS):
                matmul(state_bank[:, n * C:(n + 1) * C], flat[:, n * P:(n + 1) * P], h_nat[:, g % NHN, j, :],
                       i % CB == 0 and n == 0, True, ("state", i) if n == PAIRS - 1 else None)

        def copy_state(i):
            if i % CB == CB - 1:
                return
            wait(act, "state", i)
            wait(act, "z_O", i - 1)
            activate(S[:, i % 2, :, :], by(PAIRS, state_bank[:, :]), ACT.Copy, done=("S", i))

        def queries(i, n):
            u, k = divmod(i, UC)
            return qT[:, u % 2, n, k * P:(k + 1) * P]

        def split_h(i):
            g, j = divmod(i, GC)
            h = h_nat[:, g % NHN, j, :]
            hi, lo = (h_split[s][:, i % NSPLIT, :] for s in ("hi", "lo"))
            wait(act, "h_nat", g)
            wait(act, "z_O", i - NSPLIT)
            activate(hi, h, ACT.Copy, ("h_hi", i))
            wait(dve, "h_hi", i)
            wait(dve, "z_O", i - NSPLIT)
            tt(dve, lo, h, hi.bitcast(F32), ALU.subtract, ("h_lo", i))

        def scores(i):
            pair = take_bank(("A_E", i)), take_bank(("A_O", i))
            wait(pe, "qT", 2 * (i // UC) + 1)
            wait(pe, "kT", i)
            for n in range(PAIRS):
                q = queries(i, n)
                for odd, bank in enumerate(pair):
                    rows = slice(odd * D, (odd + 1) * D)
                    matmul(bank[:, n * P:(n + 1) * P], kT[rows, i % NKT, n, :], q[rows, :], True, True,
                           ("scores_" + "EO"[odd], i) if n == PAIRS - 1 else None)
            psum["A", 0, i], psum["A", 1, i] = pair

        def mask_scores(i, odd):
            eo, bank = "EO"[odd], psum.pop(("A", odd, i))
            wait(dve, "scores_" + eo, i)
            wait(dve, "A_hi_" + eo, i - 1)
            wait(dve, "A_lo_" + eo, i - 1)
            tt(dve, A[odd][:, :, :], by(PAIRS, bank[:, :]), causal.unsqueeze(1).broadcast_to([P, PAIRS, P]),
               ALU.mult, ("A_" + eo, i))
            wait(act, "A_" + eo, i)
            wait(act, "z_O", i - NSPLIT)
            activate(by(PAIRS, A_split["hi"][odd][:, i % NSPLIT, :]), A[odd][:, :, :], ACT.Copy, ("A_hi_" + eo, i))

        def split_scores(i, odd):
            eo = "EO"[odd]
            wait(dve, "A_hi_" + eo, i)
            wait(dve, "z_O", i - NSPLIT)
            hi, lo = (by(PAIRS, A_split[s][odd][:, i % NSPLIT, :]) for s in ("hi", "lo"))
            tt(dve, lo, A[odd][:, :, :], hi.bitcast(F32), ALU.subtract, ("A_lo_" + eo, i))

        def mix_tokens(i):
            first = i % CB == 0
            pair = take_bank(("Z_E", i)), take_bank(("Z_O", i))
            h_hi, h_lo = (h_split[s][:, i % NSPLIT, :] for s in ("hi", "lo"))
            wait(pe, "h_lo", i)
            for odd, bank in enumerate(pair):
                A_hi, A_lo = (A_split[s][odd][:, i % NSPLIT, :] for s in ("hi", "lo"))
                wait(pe, "A_lo_" + "EO"[odd], i)
                matmul(bank[:, :], h_hi, A_hi, True, False)
                matmul(bank[:, :], h_hi, A_lo, False, False)
                matmul(bank[:, :], h_lo, A_hi, False, first, ("z_" + "EO"[odd], i) if first else None)
            if not first:
                wait(pe, "S", i - 1)
                for n in range(PAIRS):
                    q = queries(i, n)
                    for odd, bank in enumerate(pair):
                        rows = slice(odd * D, (odd + 1) * D)
                        matmul(bank[:, n * P:(n + 1) * P], S[rows, (i - 1) % 2, n, :], q[rows, :],
                               False, n == PAIRS - 1, ("z_" + "EO"[odd], i) if n == PAIRS - 1 else None)
            psum["Z", i] = pair

        def copy_Z(i):
            for odd, bank in enumerate(psum.pop(("Z", i))):
                wait(act, "z_" + "EO"[odd], i)
                wait(act, "heads_" + "EO"[odd], i - 1)
                activate(Z[odd][:, :, :], by(PAIRS, bank[:, :]), ACT.Copy, done=("Z_" + "EO"[odd], i))

        def head_outputs(i, odd):
            eo = "EO"[odd]
            bank = take_bank(("O_" + eo, i))
            wait(pe, "Z_" + eo, i)
            wait(pe, "w_v")
            for n in range(PAIRS):
                matmul(bank[:, n * V:(n + 1) * V], Z[odd][:, n, :], wv[:, 2 * n + odd, :], True, True,
                       ("heads_" + eo, i) if n == PAIRS - 1 else None)
            psum["O", odd, i] = bank

        def copy_outputs(i, odd):
            wait(act, "heads_" + "EO"[odd], i)
            wait(act, "nT_psum", H * ((i - NN) // GC) + H - 1)
            wait(act, "w_g_lo")
            wait(act, "w_qk_lo")
            wait(act, "w_o_lo")
            activate(N[:, i % NN, odd, :, :], by(PAIRS, psum.pop(("O", odd, i))[:, :]), ACT.Copy, done=("O_" + "EO"[odd], i))

        def head_stats(i, odd):
            s, slot, eo = i % NGN, i % NN, "EO"[odd]
            wait(dve, "gn_apply_E", i - NGN)
            wait(dve, "gn_apply_O", i - NGN)
            wait(dve, "O_" + eo, i)
            for n in range(PAIRS):
                k = odd * PAIRS + n
                a, o = N[:, slot, odd, n, :], gn_stats[:, s, k, :]
                emit(dve, lambda e, a=a, o=o: e.bn_stats(o, a), ("gn_stats_" + eo, PAIRS * i + n))
            for n in range(PAIRS):
                k = odd * PAIRS + n
                wait(dve, "gn_stats_" + eo, PAIRS * i + n)
                a, o = gn_stats[:, s, k, :], gn_mv[:, s, k, :]
                emit(dve, lambda e, a=a, o=o: e.bn_aggr(o, a), ("gn_mv_" + eo, i) if n == PAIRS - 1 else None)

        def head_rstd(i):
            s, c = i % NGN, i % CB
            for eo in "EO":
                wait(pool, "gn_mv_" + eo, i)
            wait(pool, "gn_apply_E", i - NGN)
            wait(pool, "gn_apply_O", i - NGN)
            eps_eo = norm_eps[:, c, :].rearrange("p (a e) -> p e a", e=2)
            tt(pool, by(2, gn_var[:, s, :]), gn_mv[:, s, :, 1].rearrange("p (e a) -> p e a", e=2), eps_eo, ALU.add,
               ("gn_var", i))
            wait(pool, "gn_var", i)
            tt(pool, gn_rstd[:, s, :], gn_var[:, s, :], minus_half[:, :].broadcast_to([P, H]), ALU.pow,
               ("gn_rstd", i))

        def norm_heads_E(i):
            s, slot = i % NGN, i % NN
            wait(dve, "gn_rstd", i)
            wait(dve, "gn_apply_O", i - 1)
            stt(dve, gn_shift[:, :], gn_mv[:, s, PAIRS:H, 0], -1.0, gn_rstd[:, s, PAIRS:H], ALU.mult, ALU.mult,
                ("gn_shift", i))
            for k in range(PAIRS):
                a = N[:, slot, 0, k, :]
                ts(dve, a, a, gn_mv[:, s, k, 0:1], gn_rstd[:, s, k:k + 1], ALU.subtract, ALU.mult,
                   ("gn_apply_E", i) if k == PAIRS - 1 else None)

        def norm_heads_O(i):
            s, slot = i % NGN, i % NN
            wait(act, "gn_shift", i)
            for k in range(PAIRS):
                a = N[:, slot, 1, k, :]
                activate(a, a, ACT.Identity, ("gn_apply_O", i) if k == PAIRS - 1 else None,
                         scale=gn_rstd[:, s, PAIRS + k:PAIRS + k + 1], bias=gn_shift[:, k:k + 1])

        def project_gate(n):
            g, h = divmod(n, H)
            cols = slice(h * V, (h + 1) * V)
            hi, lo = (hT[s][:, g % NHT, :] for s in ("hi", "lo"))
            bank = take_bank(("gate", n))
            wait(pe, "w_g_lo")
            matmul(bank[:, :], wg["hi"][:, cols], hi, True, False)
            matmul(bank[:, :], wg["hi"][:, cols], lo, False, False)
            matmul(bank[:, :], wg["lo"][:, cols], hi, False, True, ("gate_psum", n))
            psum["g", n] = bank

        def gate_silu(n):
            wait(act, "gate_psum", n)
            wait(act, "y", n - 2)
            activate(gate[:, n % 2, :], psum.pop(("g", n))[:, :], ACT.Silu, ("gate", n))

        def turn_head(n):
            g, h = divmod(n, H)
            bank = take_bank(("scaled", n))
            wait(pe, "gn_apply_" + "EO"[h % 2], GC * g + GC - 1)
            for j in range(GC):
                transpose(bank[:, j * P:(j + 1) * P], N[:, (GC * g + j) % NN, h % 2, h // 2, :],
                          ("nT_psum", n) if j == GC - 1 else None)
            psum["n", n] = bank

        def scale_head(n):
            h = n % H
            wait(act, "nT_psum", n)
            wait(act, "gn")
            wait(act, "y_lo", n - NY)
            activate(scaled[:, n % NY, :], psum.pop(("n", n))[:, :], ACT.Identity, ("scaled", n),
                     bias=gn[:, 1, h:h + 1], scale=gn[:, 0, h:h + 1])

        def gate_head(n):
            q = dve if n // H == NGROUP - 1 else pool
            wait(q, "gate", n)
            wait(q, "scaled", n)
            y = scaled[:, n % NY, :]
            tt(q, y, y, gate[:, n % 2, :], ALU.mult, ("y", n))

        def split_gated_hi(n):
            wait(act, "y", n)
            wait(act, "out_head", n - 2)
            activate(y_split["hi"][:, n % 2, :], scaled[:, n % NY, :], ACT.Copy, ("y_hi", n))

        def split_gated_lo(n):
            wait(dve, "y_hi", n)
            wait(dve, "out_head", n - 2)
            tt(dve, y_split["lo"][:, n % 2, :], scaled[:, n % NY, :], y_split["hi"][:, n % 2, :].bitcast(F32),
               ALU.subtract, ("y_lo", n))

        def project_out(n):
            g, h = divmod(n, H)
            hi, lo = (y_split[s][:, n % 2, :] for s in ("hi", "lo"))
            cols = slice(h * C, (h + 1) * C)
            wait(pe, "w_o_lo")
            wait(pe, "y_lo", n)
            if h == 0:
                wait(pe, "attnT", g - 1)
            matmul(out_bank[:, :], wo["hi"][:, cols], hi, h == 0, False)
            matmul(out_bank[:, :], wo["hi"][:, cols], lo, False, False)
            matmul(out_bank[:, :], wo["lo"][:, cols], hi, False, h == H - 1, ("out_head", n))

        def scale_attn(g):
            b = g // GB
            wait(act, "out_head", H * g + H - 1)
            wait(act, "ffn_out", g - 1)
            wait(act, "mod_cols")
            activate(attn_flat, out_bank[:, :], ACT.Copy, ("attnT", g), scale=mod_cols[:, 2, b:b + 1])

        def turn_attn(g):
            bank = take_bank(("residual", g))
            wait(pe, "attnT", g)
            for j in range(GC):
                transpose(bank[:, j * P:(j + 1) * P], attn_flat[:, j * P:(j + 1) * P],
                          ("attn_psum", g) if j == GC - 1 else None)
            psum["attn", g] = bank

        def residual(g):
            xg = X[:, g % NX, :, :]
            wait(dve, "attn_psum", g)
            tt(dve, xg, xg, by(GC, psum.pop(("attn", g))[:, :]), ALU.add, ("residual", g))

        def transpose_n2(g):
            bank = take_bank(("h2T", g))
            wait(pe, "ln_apply1", g)
            for j in range(GC):
                transpose(bank[:, j * P:(j + 1) * P], normed[:, j, :], ("n2T", g) if j == GC - 1 else None)
            psum["n2", g] = bank

        def modulate2(g):
            b, half = divmod(g, GB)
            bank = psum.pop(("n2", g))
            wait(act, "n2T", g)
            wait(act, "mod_cols")
            wait(act, "mix_k", g - 2)
            wait(act, "h2T_edge", g - 1 if half == 0 else -1)
            activate(h2T[:, half, 1:1 + W], bank[:, :], ACT.Identity, ("h2T", g), bias=mod_cols[:, 0, b:b + 1],
                     scale=mod_cols[:, 1, b:b + 1])
            if half:
                wait(act, "h2T", g - 1)
                activate(h2T[:, half, 0:1], h2T[:, half - 1, W:W + 1], ACT.Copy, ("h2T_edge", g))

        def mix_shift(g):
            half = g % GB
            now, before = h2T[:, half, 1:1 + W], h2T[:, half, 0:W]
            first = dve if g == NGROUP - 1 else pool
            for q in (first, dve):
                wait(q, "h2T", g)
                if half:
                    wait(q, "h2T_edge", g)
                else:
                    wait(q, "zero_column")
            wait(first, "mix_k", g - 1)
            wait(first, "attn_psum", g)
            wait(first, "ffn_out", g - 1)
            tt(first, delta, now, before, ALU.subtract, ("delta", g))
            wait(dve, "delta", g)
            wait(dve, "mu")
            wait(dve, "rk_psum", 2 * (g - 1) + 1)
            for n, what in enumerate("rk"):
                stt(dve, mixed[what][:, :], delta, mu[:, n:n + 1], before, ALU.mult, ALU.add,
                    ("mix_" + what, g))

        def project_r(g):
            bank = take_bank(("r_tanh", g))
            wait(pe, "w_ffn")
            wait(pe, "mix_r", g)
            for j in range(GC):
                matmul(bank[:, j * C:(j + 1) * C], mixed["r"][:, j * P:(j + 1) * P], wffn[:, 0, :], True, True,
                       ("rk_psum", 2 * g) if j == GC - 1 else None)
            psum["r", g] = bank

        def act_r(g):
            wait(act, "rk_psum", 2 * g)
            wait(act, "ffn_product", g - 1)
            activate(r_tanh, by(GC, psum.pop(("r", g))[:, :]), ACT.Tanh, ("r_tanh", g), scale=0.5)

        def project_ffn_k(g):
            bank = take_bank(("relu", g))
            wait(pe, "mix_k", g)
            matmul(bank[:, :], wffn[:, 1, :], mixed["k"][:, :], True, True, ("rk_psum", 2 * g + 1))
            psum["ffn_k", g] = bank

        def act_k(g):
            wait(act, "rk_psum", 2 * g + 1)
            wait(act, "ffn_psum", g - 1)
            activate(k_act[:, :], psum.pop(("ffn_k", g))[:, :], ACT.Relu, ("relu", g))
            wait(act, "relu", g)
            activate(k_act[:, :], k_act[:, :], ACT.Square, ("k_act", g))

        def ffn_gate(g):
            m = mod[:, (g // GB) % NMOD, :, :]
            wait(dve, "r_tanh", g)
            stt(dve, r_tanh, r_tanh, 1.0, m[:, 2:3, :].broadcast_to([P, GC, C]), ALU.add, ALU.mult,
                ("r_gate", g))

        def project_ffn_out(g):
            bank = take_bank(("ffn_product", g))
            wait(pe, "k_act", g)
            for j in range(GC):
                matmul(bank[:, j * C:(j + 1) * C], k_act[:, j * P:(j + 1) * P], wffn[:, 2, :], True, True,
                       ("ffn_psum", g) if j == GC - 1 else None)
            psum["ffn", g] = bank

        def ffn_out(g):
            xg, bank = X[:, g % NX, :, :], psum.pop(("ffn", g))
            wait(dve, "ffn_psum", g)
            wait(dve, "r_gate", g)
            wait(dve, "residual", g)
            wait(dve, "ffn_out", g - 1)
            stt(dve, attn[:, :, :], by(GC, bank[:, :]), 0.5, r_tanh, ALU.mult, ALU.mult, ("ffn_product", g))
            q = dve if g == NGROUP - 1 else pool
            wait(q, "ffn_product", g)
            tt(q, xg, xg, attn[:, :, :], ALU.add, ("ffn_out", g))
            wait(sp, "ffn_out", g)
            dma(sp, out_rows[g], xg, ("out%d" % (g % NX), g // NX))

        def one(f):
            return 1, NCHUNK, f

        def group(f):
            return GC, NGROUP, f

        stages = {
            "key_tables": (1, CB, key_tables),
            "project_k": one(project_k), "rotate_k": one(rotate_k),
            "transpose_k": one(transpose_k), "copy_kT": one(copy_kT),
            "state": one(accumulate_state), "copy_state": one(copy_state),
            "split_h": one(split_h), "scores": one(scores),
            "mix": one(mix_tokens), "copy_Z": one(copy_Z), "head_rstd": one(head_rstd),
            "norm_heads_E": one(norm_heads_E), "norm_heads_O": one(norm_heads_O),
            "scale_attn": group(scale_attn), "turn_attn": group(turn_attn),
            "transpose_h": group(transpose_h), "split_hT": group(split_hT),
            "norm_stats0": group(lambda g: norm_stats(g, 0)), "norm_apply0": group(lambda g: norm_apply(g, 0)),
            "modulate": group(modulate),
            "mod_input": (GB * GC, B, mod_input), "mod_rows": (GB * GC, B, mod_rows),
            "residual": group(residual), "norm_stats1": group(lambda g: norm_stats(g, 1)),
            "norm_apply1": group(lambda g: norm_apply(g, 1)), "transpose_n2": group(transpose_n2),
            "modulate2": group(modulate2), "mix_shift": group(mix_shift), "project_r": group(project_r),
            "act_r": group(act_r), "project_ffn_k": group(project_ffn_k), "act_k": group(act_k),
            "ffn_gate": group(ffn_gate), "project_ffn_out": group(project_ffn_out), "ffn_out": group(ffn_out),
            "load_x": (GC, NGROUP - NX, lambda g: load_x(g + NX)),
        }
        for n in range(2):
            for name, f in (("project_q", project_q), ("rotate_q", rotate_q)):
                stages[f"{name}_{n}"] = (UC, NCHUNK // UC, lambda u, f=f, n=n: f(u, n))
            for name, f in (("mask", mask_scores), ("split", split_scores), ("head_outputs", head_outputs),
                            ("copy_outputs", copy_outputs), ("head_stats", head_stats)):
                stages[f"{name}_{'EO'[n]}"] = one(lambda i, f=f, n=n: f(i, n))
            for name, f in (("project_gate", project_gate), ("gate_silu", gate_silu), ("turn_head", turn_head),
                            ("scale_head", scale_head), ("gate_head", gate_head), ("split_y_hi", split_gated_hi),
                            ("split_y_lo", split_gated_lo), ("project_out", project_out)):
                stages[f"{name}_{n}"] = (1, NCHUNK, lambda i, f=f, n=n: f(2 * i + n))

        queued = dict.fromkeys(stages, 0)

        def queue(name):
            queued[name] += 1
            stages[name][2](queued[name] - 1)

        prologue_loads()
        prologue()
        for name in PROLOGUE:
            if name in stages:
                queue(name)
            elif name == "mod_columns":
                mod_columns()
            elif name == "split_w_qk":
                split_weights("w_qk", raw_qk, wqk)
            elif name == "split_w_o":
                split_weights("w_o", raw_o, wo)
            elif name == "split_w_g":
                split_weights("w_g", raw_g, wg)
        last = max(lag + stages[name][0] * (stages[name][1] - 1) for name, lag in TAIL_ORDER)
        for step in range(min(lag for name, lag in HEAD_ORDER), last + 1):
            order = HEAD_ORDER if step < HEAD_END else ORDER if step < TAIL_START else TAIL_ORDER
            for name, lag in order:
                every, many, _ = stages[name]
                while queued[name] < min(many, (step - lag) // every + 1):
                    queue(name)
        assert all(queued[name] == many for name, (_, many, _) in stages.items())
        for g in range(max(0, NGROUP - NX), NGROUP):
            wait_stored(g)

        block = ctx.enter_context(nc.Block())

        @block.tensor
        def _(e):
            for f in pe:
                f(e)

        @block.scalar
        def _(e):
            for f in act:
                f(e)

        @block.vector
        def _(e):
            for f in dve:
                f(e)

        @block.gpsimd
        def _(e):
            for f in pool:
                f(e)

        @block.sync
        def _(e):
            for f in sp:
                f(e)


def kernel(L0_attn_x, L0_attn_Wq, L0_attn_Wk, L0_attn_Wv, L0_attn_Wg, L0_attn_Wo, L0_attn_gn_weight,
           L0_attn_gn_bias, L0_ffn_W_r, L0_ffn_W_k, L0_ffn_W_v, L0_ffn_mu_r, L0_ffn_mu_k, L0_c, L0_wmod):
    import concourse.bacc as bacc
    from concourse.bass_utils import run_bass_kernel_spmd

    def a(v):
        return np.asarray(v)

    def quarters(w):
        return w.reshape(H, 2, 2, QUARTER, C).transpose(0, 2, 1, 3, 4).reshape(H * D, C)

    lay = np.ascontiguousarray
    const, const_q = constants()
    arrays = {
        "x": lay(a(L0_attn_x)),
        "cT": lay(a(L0_c).T),
        "w_mod": lay(a(L0_wmod)),
        "w_qkT": lay(np.concatenate([quarters(a(L0_attn_Wq)), quarters(a(L0_attn_Wk))], 0).T),
        "w_gT": lay(a(L0_attn_Wg).T),
        "w_vT": lay(a(L0_attn_Wv).T),
        "w_oT": lay(a(L0_attn_Wo).T.reshape(H, V, C).transpose(1, 0, 2).reshape(V, H * C)),
        "norm_wb": lay(np.stack([a(L0_attn_gn_weight), a(L0_attn_gn_bias)]).reshape(2, H, V).transpose(2, 0, 1)),
        "w_ffnT": lay(np.concatenate([a(L0_ffn_W_r).T, a(L0_ffn_W_k).T, a(L0_ffn_W_v).T], 1)),
        "ffn_mu": lay(np.stack([a(L0_ffn_mu_r), a(L0_ffn_mu_k)], 1)),
        "const": const,
        "const_q": const_q,
    }
    nc = bacc.Bacc("TRN2", target_bir_lowering=False, num_devices=1)
    ins = [nc.dram_tensor("in_" + n, v.shape, mybir.dt.from_np(v.dtype), kind="ExternalInput").ap()
           for n, v in arrays.items()]
    out = nc.dram_tensor("out", (B, T, C), F32, kind="ExternalOutput").ap()
    build(nc, *ins, out)
    r = run_bass_kernel_spmd(nc, [{"in_" + n: v for n, v in arrays.items()}], core_ids=[0])
    return r.results[0]["out"]
```
